# Optimizing a Trainium2 kernel written in Bass

```python
import numpy as np
import jax
import jax.numpy as jnp

def _softmax(x, axis=-1):
    return jax.nn.softmax(x, axis=axis)

def _gelu(x):
    return jax.nn.gelu(x, approximate=True)

def _silu(x):
    return jax.nn.silu(x)

def _sigmoid(x):
    return jax.nn.sigmoid(x)

def _layernorm(x, axis=-1, eps=1e-05):
    m = jnp.mean(x, axis=axis, keepdims=True)
    v = jnp.var(x, axis=axis, keepdims=True)
    return (x - m) / jnp.sqrt(v + eps)

def _scatter_add(tgt, idx, src, axis=0):
    return tgt.at[idx].add(src)

def _segment_sum(src, seg, n):
    return jax.ops.segment_sum(src, seg, n)
kernel_name = 'mk_flamingo_gated_d4_seqx_r8_32d3bf'

def setup_inputs(seed: int=0):
    np.random.seed(seed)
    _w = jnp.asarray

    def _rec_inputs():
        import jax
        import jax.numpy as jnp
        _rk = jax.random.key(seed)
        x = 7.22e-05 + 1 * jax.random.normal(jax.random.fold_in(_rk, 1), (8, 128, 512), jnp.float32)
        _lenS = 128 - jax.random.randint(jax.random.fold_in(_rk, 7), (8,), 0, max(1, 128 // 4) + 1, jnp.int32)
        _lenS2 = 128 - jax.random.randint(jax.random.fold_in(_rk, 8), (8,), 0, max(1, 128 // 4) + 1, jnp.int32)
        _ctx_4096P = jax.random.normal(jax.random.fold_in(_rk, 11), (8, 16, 512), jnp.float32)
        _ctx_4096c = jax.random.dirichlet(jax.random.fold_in(_rk, 511), 0.3 * jnp.ones((16,), jnp.float32), (8, 128))
        _ctx_4096t = jnp.einsum('bsk,bkd->bsd', _ctx_4096c, _ctx_4096P)
        _ctx_4096t = _ctx_4096t * jax.lax.rsqrt(jnp.mean(jnp.square(_ctx_4096t)) + 1e-12) * 0.953939
        ctx_4096 = 4.13588e-05 + 0.999923 * (_ctx_4096t + 0.3 * jax.random.normal(jax.random.fold_in(_rk, 611), (8, 128, 512), jnp.float32))
        _validS = jnp.arange(128)[None, :] < _lenS[:, None]
        _validS2 = jnp.arange(128)[None, :] < _lenS2[:, None]
        _causal = jnp.tril(jnp.ones((128, 128), dtype=bool))
        mask_BxSxS2_bk0 = jnp.logical_not(jnp.broadcast_to(_validS2[:, None, :], (8, 128, 128)))
        mask_1x1xSxS2_ff0 = jnp.where(jnp.ones((1, 1, 128, 128), dtype=bool), 0.0, -1000000000.0).astype(jnp.float32)
        _g = jax.random.normal(jax.random.fold_in(_rk, 9001), (2, 4), jnp.float32)
        _g = jnp.sign(_g) * jnp.maximum(jnp.abs(_g), 1.0) + (_g == 0) * 1.0
        g_xattn = _g[0]
        g_ffn = _g[1]
        return (x, ctx_4096, mask_BxSxS2_bk0, mask_1x1xSxS2_ff0, g_xattn, g_ffn)
    x, ctx_4096, mask_BxSxS2_bk0, mask_1x1xSxS2_ff0, g_xattn, g_ffn = _rec_inputs()

    def _L0_xattn_setup():
        import jax, jax.numpy as jnp
        import numpy as np
        DIM = 512
        NUM_HEADS = 32
        NUM_KV_HEADS = 8
        HEAD_DIM = DIM // NUM_HEADS
        KV_DIM = DIM // (NUM_HEADS // NUM_KV_HEADS)
        B, S = (1, 256)
        key = jax.random.key(seed)
        ks = jax.random.split(key, 7)
        w_scale = DIM ** (-0.5)
        return {'query': jax.random.normal(ks[0], (B, S, DIM), jnp.float32), 'key': jax.random.normal(ks[1], (B, S, DIM), jnp.float32), 'value': jax.random.normal(ks[2], (B, S, DIM), jnp.float32), 'Wq': jax.random.normal(ks[3], (DIM, DIM), jnp.float32) * w_scale, 'Wk': jax.random.normal(ks[4], (DIM, KV_DIM), jnp.float32) * w_scale, 'Wv': jax.random.normal(ks[5], (DIM, KV_DIM), jnp.float32) * w_scale, 'Wo': jax.random.normal(ks[6], (DIM, DIM), jnp.float32) * w_scale}
    _L0_xattn_all = _L0_xattn_setup()
    _L0_xattn_in = {k: v for k, v in _L0_xattn_all.items() if k in ('Wq', 'Wk', 'Wv', 'Wo')}
    del _L0_xattn_all

    def _L0_ffn_setup():
        import jax, jax.numpy as jnp
        import numpy as np
        ALPHA = 32
        R = 16
        SCALING = ALPHA / R
        key = jax.random.key(seed)
        k1, k2, k3, k4 = jax.random.split(key, 4)
        B_, S, D = (4, 256, 512)
        H, r, O = (8, R, 512)
        x = jax.random.normal(k1, (B_, S, D), dtype=jnp.float32)
        A = jax.random.normal(k2, (H, r, D), dtype=jnp.float32) * 0.02
        Bm = jax.random.normal(k3, (H, O, r), dtype=jnp.float32) * 0.02
        Wr = jax.random.normal(k4, (H, D), dtype=jnp.float32) * 0.02
        br = jnp.zeros((H,), dtype=jnp.float32)
        return {'x': x, 'A': A, 'B': Bm, 'Wr': Wr, 'br': br}
    _L0_ffn_all = _L0_ffn_setup()
    _L0_ffn_in = {k: v for k, v in _L0_ffn_all.items() if k in ('A', 'B', 'Wr', 'br')}
    del _L0_ffn_all

    def _L1_xattn_setup():
        import jax, jax.numpy as jnp
        import numpy as np
        B, LQ, LK, D, H, DH = (2, 128, 128, 512, 32, 128)
        EPS = 1e-05

        def _rmsnorm(x, weight):
            var = jnp.mean(jnp.square(x), axis=-1, keepdims=True)
            return x * jax.lax.rsqrt(var + EPS) * weight
        key = jax.random.key(seed)
        ks = jax.random.split(key, 8)
        scale = 0.02
        return {'hidden_states': jax.random.normal(ks[0], (B, LQ, D), jnp.float32), 'key_value_states': jax.random.normal(ks[1], (B, LK, D), jnp.float32), 'attention_mask': jax.random.randint(ks[2], (B, LQ, LK), 0, 2) > 0, 'position_bias': jax.random.normal(ks[3], (H, LQ, LK), jnp.float32), 'ln_weight': jnp.ones((D,), jnp.float32), 'w_q': jax.random.normal(ks[4], (H * DH, D), jnp.float32) * scale, 'w_k': jax.random.normal(ks[5], (H * DH, D), jnp.float32) * scale, 'w_v': jax.random.normal(ks[6], (H * DH, D), jnp.float32) * scale, 'w_out': jax.random.normal(ks[7], (D, H * DH), jnp.float32) * scale}
    _L1_xattn_all = _L1_xattn_setup()
    _L1_xattn_in = {k: v for k, v in _L1_xattn_all.items() if k in ('position_bias', 'ln_weight', 'w_q', 'w_k', 'w_v', 'w_out')}
    del _L1_xattn_all

    def _L1_ffn_setup():
        import jax, jax.numpy as jnp
        import numpy as np
        E = 8
        R = 8
        DIN = 512
        DOUT = 512
        TOP_K = 2
        SCALING = 2.0

        def _moe_lora(xf, gate_W, A, B):
            gate_probs = jax.nn.softmax(xf @ gate_W.T, axis=-1)
            weights, sel = jax.lax.top_k(gate_probs, TOP_K)
            weights = weights / jnp.sum(weights, axis=-1, keepdims=True)
            T = xf.shape[0]
            w_dense = jnp.zeros((T, E), xf.dtype).at[jnp.arange(T)[:, None], sel].add(weights)
            h = jnp.einsum('td,erd->ter', xf, A)
            h = h * (w_dense[:, :, None] * SCALING)
            return jnp.einsum('ter,eor->to', h, B)
        key = jax.random.key(seed)
        k0, k1, k2, k3, k4 = jax.random.split(key, 5)
        x = jax.random.normal(k0, (4, 256, DIN), jnp.float32)
        W_base = jax.random.normal(k1, (DOUT, DIN), jnp.float32) * 0.02
        gate_W = jax.random.normal(k2, (E, DIN), jnp.float32) * 0.02
        A = jax.random.normal(k3, (E, R, DIN), jnp.float32) * 0.02
        B = jax.random.normal(k4, (E, DOUT, R), jnp.float32) * 0.02
        return {'x': x, 'W_base': W_base, 'gate_W': gate_W, 'A': A, 'B': B}
    _L1_ffn_all = _L1_ffn_setup()
    _L1_ffn_in = {k: v for k, v in _L1_ffn_all.items() if k in ('W_base', 'gate_W', 'A', 'B')}
    del _L1_ffn_all

    def _L2_xattn_setup():
        import jax, jax.numpy as jnp
        import numpy as np
        NUM_HEADS = 32
        NUM_KV_HEADS = 8
        HEAD_DIM = 128
        HIDDEN = 512
        EPS = 1e-05

        def rmsnorm(x, w, eps=EPS):
            xf = x.astype(jnp.float32)
            var = jnp.mean(xf * xf, axis=-1, keepdims=True)
            return w * (xf * jax.lax.rsqrt(var + eps)).astype(x.dtype)
        key = jax.random.key(seed)
        ks = jax.random.split(key, 10)
        B, Q, KV = (1, 128, 6404)
        s = 1.0 / np.sqrt(HIDDEN)
        return {'hidden_states': jax.random.normal(ks[0], (B, Q, HIDDEN), jnp.float32), 'cross_attention_states': jax.random.normal(ks[1], (B, KV, HIDDEN), jnp.float32), 'attention_mask': jnp.zeros((B, 1, Q, KV), jnp.float32), 'q_proj_w': jax.random.normal(ks[2], (NUM_HEADS * HEAD_DIM, HIDDEN), jnp.float32) * s, 'k_proj_w': jax.random.normal(ks[3], (NUM_KV_HEADS * HEAD_DIM, HIDDEN), jnp.float32) * s, 'v_proj_w': jax.random.normal(ks[4], (NUM_KV_HEADS * HEAD_DIM, HIDDEN), jnp.float32) * s, 'o_proj_w': jax.random.normal(ks[5], (HIDDEN, NUM_HEADS * HEAD_DIM), jnp.float32) * s, 'q_norm_w': jnp.ones((HEAD_DIM,), jnp.float32), 'k_norm_w': jnp.ones((HEAD_DIM,), jnp.float32)}
    _L2_xattn_all = _L2_xattn_setup()
    _L2_xattn_in = {k: v for k, v in _L2_xattn_all.items() if k in ('q_proj_w', 'k_proj_w', 'v_proj_w', 'o_proj_w', 'q_norm_w', 'k_norm_w')}
    del _L2_xattn_all

    def _L2_ffn_setup():
        import jax, jax.numpy as jnp
        import numpy as np
        D_MODEL = 512
        D_HIDDEN = 1376
        RANK = 16
        BATCH, SEQ = (2, 256)

        def _matmul_lora(x, w, a, b, scale=1.0):
            out = jnp.einsum('bsd,hd->bsh', x, w)
            out = out + jnp.einsum('bsr,hr->bsh', jnp.einsum('bsd,rd->bsr', x, a), b) * scale
            return out
        key = jax.random.key(seed)
        ks = jax.random.split(key, 10)
        s = 0.02
        return {'x': jax.random.normal(ks[0], (BATCH, SEQ, D_MODEL), jnp.float32), 'gate_w': jax.random.normal(ks[1], (D_HIDDEN, D_MODEL), jnp.float32) * s, 'up_w': jax.random.normal(ks[2], (D_HIDDEN, D_MODEL), jnp.float32) * s, 'down_w': jax.random.normal(ks[3], (D_MODEL, D_HIDDEN), jnp.float32) * s, 'gate_a': jax.random.normal(ks[4], (RANK, D_MODEL), jnp.float32) * s, 'gate_b': jax.random.normal(ks[5], (D_HIDDEN, RANK), jnp.float32) * s, 'up_a': jax.random.normal(ks[6], (RANK, D_MODEL), jnp.float32) * s, 'up_b': jax.random.normal(ks[7], (D_HIDDEN, RANK), jnp.float32) * s, 'down_a': jax.random.normal(ks[8], (RANK, D_HIDDEN), jnp.float32) * s, 'down_b': jax.random.normal(ks[9], (D_MODEL, RANK), jnp.float32) * s}
    _L2_ffn_all = _L2_ffn_setup()
    _L2_ffn_in = {k: v for k, v in _L2_ffn_all.items() if k in ('gate_w', 'up_w', 'down_w', 'gate_a', 'gate_b', 'up_a', 'up_b', 'down_a', 'down_b')}
    del _L2_ffn_all

    def _L3_xattn_setup():
        import jax, jax.numpy as jnp
        import numpy as np
        import math
        HIDDEN = 512
        N_HEADS = 32
        HEAD_DIM = 128
        N_KV_HEADS = 4
        N_GROUPS = N_HEADS // N_KV_HEADS
        key = jax.random.key(seed)
        ks = jax.random.split(key, 6)
        B, NL, S = (8, 64, 512)
        latents = jax.random.normal(ks[0], (B, NL, HIDDEN), dtype=jnp.float32)
        context = jax.random.normal(ks[1], (B, S, HIDDEN), dtype=jnp.float32)
        scale = 1.0 / math.sqrt(HIDDEN)
        Wq = jax.random.normal(ks[2], (HIDDEN, N_HEADS * HEAD_DIM), dtype=jnp.float32) * scale
        Wk = jax.random.normal(ks[3], (HIDDEN, N_KV_HEADS * HEAD_DIM), dtype=jnp.float32) * scale
        Wv = jax.random.normal(ks[4], (HIDDEN, N_KV_HEADS * HEAD_DIM), dtype=jnp.float32) * scale
        Wo = jax.random.normal(ks[5], (N_HEADS * HEAD_DIM, HIDDEN), dtype=jnp.float32) * scale
        return {'latents': latents, 'context': context, 'Wq': Wq, 'Wk': Wk, 'Wv': Wv, 'Wo': Wo}
    _L3_xattn_all = _L3_xattn_setup()
    _L3_xattn_in = {k: v for k, v in _L3_xattn_all.items() if k in ('Wq', 'Wk', 'Wv', 'Wo')}
    del _L3_xattn_all

    def _L3_ffn_setup():
        import jax, jax.numpy as jnp
        import numpy as np
        IN_FEATURES = 512

        def _dequantize(qweight, scale, zero_point):
            N, K_packed = qweight.shape
            groups = K_packed // 3
            p = qweight.reshape(N, groups, 3)
            v0 = p[:, :, 0] & 63
            v1 = p[:, :, 0] >> 6 & 63
            v2 = p[:, :, 1] & 63
            v3 = p[:, :, 2] & 63
            unpacked = jnp.stack([v0, v1, v2, v3], axis=2).reshape(N, groups * 4)
            unpacked = unpacked[:, :IN_FEATURES]
            return (unpacked.astype(jnp.float32) - zero_point) * scale
        key = jax.random.key(seed)
        k1, k2, k3, k4, k5 = jax.random.split(key, 5)
        x = jax.random.normal(k1, (8, 256, 512), dtype=jnp.float32)
        qweight = jax.random.randint(k2, (512, 384), 0, 512, dtype=jnp.int32)
        weight_scale = jax.random.uniform(k3, (512, 1), dtype=jnp.float32) * 0.02 + 0.001
        weight_zero_point = jax.random.uniform(k4, (512, 1), dtype=jnp.float32) * 63.0
        bias = jax.random.normal(k5, (512,), dtype=jnp.float32)
        return {'x': x, 'qweight': qweight, 'weight_scale': weight_scale, 'weight_zero_point': weight_zero_point, 'bias': bias}
    _L3_ffn_all = _L3_ffn_setup()
    _L3_ffn_in = {k: v for k, v in _L3_ffn_all.items() if k in ('qweight', 'weight_scale', 'weight_zero_point', 'bias')}
    del _L3_ffn_all
    return {'x': x, 'ctx_4096': ctx_4096, 'mask_BxSxS2_bk0': mask_BxSxS2_bk0, 'mask_1x1xSxS2_ff0': mask_1x1xSxS2_ff0, 'g_xattn': g_xattn, 'g_ffn': g_ffn, 'L0_xattn_Wq': _L0_xattn_in['Wq'], 'L0_xattn_Wk': _L0_xattn_in['Wk'], 'L0_xattn_Wv': _L0_xattn_in['Wv'], 'L0_xattn_Wo': _L0_xattn_in['Wo'], 'L0_ffn_A': _L0_ffn_in['A'], 'L0_ffn_B': _L0_ffn_in['B'], 'L0_ffn_Wr': _L0_ffn_in['Wr'], 'L0_ffn_br': _L0_ffn_in['br'], 'L1_xattn_position_bias': _L1_xattn_in['position_bias'], 'L1_xattn_ln_weight': _L1_xattn_in['ln_weight'], 'L1_xattn_w_q': _L1_xattn_in['w_q'], 'L1_xattn_w_k': _L1_xattn_in['w_k'], 'L1_xattn_w_v': _L1_xattn_in['w_v'], 'L1_xattn_w_out': _L1_xattn_in['w_out'], 'L1_ffn_W_base': _L1_ffn_in['W_base'], 'L1_ffn_gate_W': _L1_ffn_in['gate_W'], 'L1_ffn_A': _L1_ffn_in['A'], 'L1_ffn_B': _L1_ffn_in['B'], 'L2_xattn_q_proj_w': _L2_xattn_in['q_proj_w'], 'L2_xattn_k_proj_w': _L2_xattn_in['k_proj_w'], 'L2_xattn_v_proj_w': _L2_xattn_in['v_proj_w'], 'L2_xattn_o_proj_w': _L2_xattn_in['o_proj_w'], 'L2_xattn_q_norm_w': _L2_xattn_in['q_norm_w'], 'L2_xattn_k_norm_w': _L2_xattn_in['k_norm_w'], 'L2_ffn_gate_w': _L2_ffn_in['gate_w'], 'L2_ffn_up_w': _L2_ffn_in['up_w'], 'L2_ffn_down_w': _L2_ffn_in['down_w'], 'L2_ffn_gate_a': _L2_ffn_in['gate_a'], 'L2_ffn_gate_b': _L2_ffn_in['gate_b'], 'L2_ffn_up_a': _L2_ffn_in['up_a'], 'L2_ffn_up_b': _L2_ffn_in['up_b'], 'L2_ffn_down_a': _L2_ffn_in['down_a'], 'L2_ffn_down_b': _L2_ffn_in['down_b'], 'L3_xattn_Wq': _L3_xattn_in['Wq'], 'L3_xattn_Wk': _L3_xattn_in['Wk'], 'L3_xattn_Wv': _L3_xattn_in['Wv'], 'L3_xattn_Wo': _L3_xattn_in['Wo'], 'L3_ffn_qweight': _L3_ffn_in['qweight'], 'L3_ffn_weight_scale': _L3_ffn_in['weight_scale'], 'L3_ffn_weight_zero_point': _L3_ffn_in['weight_zero_point'], 'L3_ffn_bias': _L3_ffn_in['bias']}

def reference(x, ctx_4096, mask_BxSxS2_bk0, mask_1x1xSxS2_ff0, g_xattn, g_ffn, L0_xattn_Wq, L0_xattn_Wk, L0_xattn_Wv, L0_xattn_Wo, L0_ffn_A, L0_ffn_B, L0_ffn_Wr, L0_ffn_br, L1_xattn_position_bias, L1_xattn_ln_weight, L1_xattn_w_q, L1_xattn_w_k, L1_xattn_w_v, L1_xattn_w_out, L1_ffn_W_base, L1_ffn_gate_W, L1_ffn_A, L1_ffn_B, L2_xattn_q_proj_w, L2_xattn_k_proj_w, L2_xattn_v_proj_w, L2_xattn_o_proj_w, L2_xattn_q_norm_w, L2_xattn_k_norm_w, L2_ffn_gate_w, L2_ffn_up_w, L2_ffn_down_w, L2_ffn_gate_a, L2_ffn_gate_b, L2_ffn_up_a, L2_ffn_up_b, L2_ffn_down_a, L2_ffn_down_b, L3_xattn_Wq, L3_xattn_Wk, L3_xattn_Wv, L3_xattn_Wo, L3_ffn_qweight, L3_ffn_weight_scale, L3_ffn_weight_zero_point, L3_ffn_bias):
    import jax
    import jax.numpy as jnp

    def _L0_xattn_ref(query, key, value, Wq, Wk, Wv, Wo):
        import jax, jax.numpy as jnp
        import numpy as np
        DIM = 512
        NUM_HEADS = 32
        NUM_KV_HEADS = 8
        HEAD_DIM = DIM // NUM_HEADS
        KV_DIM = DIM // (NUM_HEADS // NUM_KV_HEADS)
        B, S = (1, 256)
        b, sq, _ = query.shape
        _, sk, _ = key.shape
        rep = NUM_HEADS // NUM_KV_HEADS
        q = (query @ Wq).reshape(b, sq, NUM_HEADS, HEAD_DIM).transpose(0, 2, 1, 3)
        k = (key @ Wk).reshape(b, sk, NUM_KV_HEADS, HEAD_DIM).transpose(0, 2, 1, 3)
        v = (value @ Wv).reshape(b, sk, NUM_KV_HEADS, HEAD_DIM).transpose(0, 2, 1, 3)
        k = jnp.repeat(k, rep, axis=1)
        v = jnp.repeat(v, rep, axis=1)
        scale = HEAD_DIM ** (-0.5)
        scores = jnp.einsum('bhqd,bhkd->bhqk', q, k) * scale
        probs = jax.nn.softmax(scores, axis=-1)
        out = jnp.einsum('bhqk,bhkd->bhqd', probs, v)
        out = out.transpose(0, 2, 1, 3).reshape(b, sq, DIM)
        return out @ Wo

    def _L0_ffn_ref(x, A, B, Wr, br):
        import jax, jax.numpy as jnp
        import numpy as np
        ALPHA = 32
        R = 16
        SCALING = ALPHA / R
        H = A.shape[0]
        router_logits = jnp.einsum('bsd,hd->bsh', x, Wr) + br
        scores = H * jax.nn.softmax(router_logits, axis=-1)
        low = jnp.einsum('bsd,hrd->bshr', x, A)
        out = jnp.einsum('bshr,hor,bsh->bso', low, B, scores)
        return SCALING * out

    def _L1_xattn_ref(hidden_states, key_value_states, attention_mask, position_bias, ln_weight, w_q, w_k, w_v, w_out):
        import jax, jax.numpy as jnp
        import numpy as np
        B, LQ, LK, D, H, DH = (2, 128, 128, 512, 32, 128)
        EPS = 1e-05

        def _rmsnorm(x, weight):
            var = jnp.mean(jnp.square(x), axis=-1, keepdims=True)
            return x * jax.lax.rsqrt(var + EPS) * weight
        x = _rmsnorm(hidden_states, ln_weight)
        b, lq, _ = x.shape
        lk = key_value_states.shape[1]
        h_q = (x @ w_q.T).reshape(b, lq, H, DH)
        h_k = (key_value_states @ w_k.T).reshape(b, lk, H, DH)
        h_v = (key_value_states @ w_v.T).reshape(b, lk, H, DH)
        score = jnp.einsum('bqhd,bkhd->bhqk', h_q, h_k)
        score = score + position_bias[None]
        m = attention_mask[:, None]
        score = jnp.where(m, score, -jnp.inf)
        score = jax.nn.softmax(score, axis=-1)
        score = jnp.where(m, score, 0.0)
        attn = jnp.einsum('bhqk,bkhd->bqhd', score, h_v).reshape(b, lq, H * DH)
        out = attn @ w_out.T
        return hidden_states + out

    def _L1_ffn_ref(x, W_base, gate_W, A, B):
        import jax, jax.numpy as jnp
        import numpy as np
        E = 8
        R = 8
        DIN = 512
        DOUT = 512
        TOP_K = 2
        SCALING = 2.0

        def _moe_lora(xf, gate_W, A, B):
            gate_probs = jax.nn.softmax(xf @ gate_W.T, axis=-1)
            weights, sel = jax.lax.top_k(gate_probs, TOP_K)
            weights = weights / jnp.sum(weights, axis=-1, keepdims=True)
            T = xf.shape[0]
            w_dense = jnp.zeros((T, E), xf.dtype).at[jnp.arange(T)[:, None], sel].add(weights)
            h = jnp.einsum('td,erd->ter', xf, A)
            h = h * (w_dense[:, :, None] * SCALING)
            return jnp.einsum('ter,eor->to', h, B)
        xf = x.reshape(-1, x.shape[-1])
        out = xf @ W_base.T + _moe_lora(xf, gate_W, A, B)
        return out.reshape(*x.shape[:-1], DOUT)

    def _L2_xattn_ref(hidden_states, cross_attention_states, attention_mask, q_proj_w, k_proj_w, v_proj_w, o_proj_w, q_norm_w, k_norm_w):
        import jax, jax.numpy as jnp
        import numpy as np
        NUM_HEADS = 32
        NUM_KV_HEADS = 8
        HEAD_DIM = 128
        HIDDEN = 512
        EPS = 1e-05

        def rmsnorm(x, w, eps=EPS):
            xf = x.astype(jnp.float32)
            var = jnp.mean(xf * xf, axis=-1, keepdims=True)
            return w * (xf * jax.lax.rsqrt(var + eps)).astype(x.dtype)
        B, Q, _ = hidden_states.shape
        KV = cross_attention_states.shape[1]
        n_rep = NUM_HEADS // NUM_KV_HEADS
        q = (hidden_states @ q_proj_w.T).reshape(B, Q, NUM_HEADS, HEAD_DIM).transpose(0, 2, 1, 3)
        k = (cross_attention_states @ k_proj_w.T).reshape(B, KV, NUM_KV_HEADS, HEAD_DIM).transpose(0, 2, 1, 3)
        v = (cross_attention_states @ v_proj_w.T).reshape(B, KV, NUM_KV_HEADS, HEAD_DIM).transpose(0, 2, 1, 3)
        q = rmsnorm(q, q_norm_w)
        k = jnp.repeat(k, n_rep, axis=1)
        v = jnp.repeat(v, n_rep, axis=1)
        k = rmsnorm(k, k_norm_w)
        scale = 1.0 / np.sqrt(HEAD_DIM)
        scores = jnp.einsum('bhqd,bhkd->bhqk', q, k) * scale + attention_mask
        attn = jax.nn.softmax(scores.astype(jnp.float32), axis=-1).astype(q.dtype)
        out = jnp.einsum('bhqk,bhkd->bhqd', attn, v)
        out = out.transpose(0, 2, 1, 3).reshape(B, Q, NUM_HEADS * HEAD_DIM)
        return out @ o_proj_w.T

    def _L2_ffn_ref(x, gate_w, up_w, down_w, gate_a, gate_b, up_a, up_b, down_a, down_b):
        import jax, jax.numpy as jnp
        import numpy as np
        D_MODEL = 512
        D_HIDDEN = 1376
        RANK = 16
        BATCH, SEQ = (2, 256)

        def _matmul_lora(x, w, a, b, scale=1.0):
            out = jnp.einsum('bsd,hd->bsh', x, w)
            out = out + jnp.einsum('bsr,hr->bsh', jnp.einsum('bsd,rd->bsr', x, a), b) * scale
            return out
        gate = _matmul_lora(x, gate_w, gate_a, gate_b)
        up = _matmul_lora(x, up_w, up_a, up_b)
        hidden = jax.nn.silu(gate) * up
        out = _matmul_lora(hidden, down_w, down_a, down_b)
        return out

    def _L3_xattn_ref(latents, context, Wq, Wk, Wv, Wo):
        import jax, jax.numpy as jnp
        import numpy as np
        import math
        HIDDEN = 512
        N_HEADS = 32
        HEAD_DIM = 128
        N_KV_HEADS = 4
        N_GROUPS = N_HEADS // N_KV_HEADS
        b, q_len, _ = latents.shape
        kv_len = q_len + context.shape[1]
        hidden_states = jnp.concatenate([context, latents], axis=1)
        q = (latents @ Wq).reshape(b, q_len, N_KV_HEADS, N_GROUPS, HEAD_DIM)
        k = (hidden_states @ Wk).reshape(b, kv_len, N_KV_HEADS, HEAD_DIM)
        v = (hidden_states @ Wv).reshape(b, kv_len, N_KV_HEADS, HEAD_DIM)
        scale = 1.0 / math.sqrt(HEAD_DIM)
        scores = jnp.einsum('bqhgd,bkhd->bhgqk', q, k) * scale
        attn = jax.nn.softmax(scores.astype(jnp.float32), axis=-1).astype(q.dtype)
        out = jnp.einsum('bhgqk,bkhd->bqhgd', attn, v)
        out = out.reshape(b, q_len, N_HEADS * HEAD_DIM)
        return out @ Wo

    def _L3_ffn_ref(x, qweight, weight_scale, weight_zero_point, bias):
        import jax, jax.numpy as jnp
        import numpy as np
        IN_FEATURES = 512

        def _dequantize(qweight, scale, zero_point):
            N, K_packed = qweight.shape
            groups = K_packed // 3
            p = qweight.reshape(N, groups, 3)
            v0 = p[:, :, 0] & 63
            v1 = p[:, :, 0] >> 6 & 63
            v2 = p[:, :, 1] & 63
            v3 = p[:, :, 2] & 63
            unpacked = jnp.stack([v0, v1, v2, v3], axis=2).reshape(N, groups * 4)
            unpacked = unpacked[:, :IN_FEATURES]
            return (unpacked.astype(jnp.float32) - zero_point) * scale
        w = _dequantize(qweight, weight_scale, weight_zero_point)
        return jnp.einsum('bsk,nk->bsn', x, w) + bias
    x = x + jnp.tanh(g_xattn[0]) * _L0_xattn_ref(_layernorm(x, axis=-1), ctx_4096, ctx_4096, L0_xattn_Wq, L0_xattn_Wk, L0_xattn_Wv, L0_xattn_Wo)
    x = x + jnp.tanh(g_ffn[0]) * _L0_ffn_ref(_layernorm(x, axis=-1), L0_ffn_A, L0_ffn_B, L0_ffn_Wr, L0_ffn_br)
    x = x + jnp.tanh(g_xattn[1]) * _L1_xattn_ref(_layernorm(x, axis=-1), ctx_4096, mask_BxSxS2_bk0, L1_xattn_position_bias, L1_xattn_ln_weight, L1_xattn_w_q, L1_xattn_w_k, L1_xattn_w_v, L1_xattn_w_out)
    x = x + jnp.tanh(g_ffn[1]) * _L1_ffn_ref(_layernorm(x, axis=-1), L1_ffn_W_base, L1_ffn_gate_W, L1_ffn_A, L1_ffn_B)
    x = x + jnp.tanh(g_xattn[2]) * _L2_xattn_ref(_layernorm(x, axis=-1), ctx_4096, mask_1x1xSxS2_ff0, L2_xattn_q_proj_w, L2_xattn_k_proj_w, L2_xattn_v_proj_w, L2_xattn_o_proj_w, L2_xattn_q_norm_w, L2_xattn_k_norm_w)
    x = x + jnp.tanh(g_ffn[2]) * _L2_ffn_ref(_layernorm(x, axis=-1), L2_ffn_gate_w, L2_ffn_up_w, L2_ffn_down_w, L2_ffn_gate_a, L2_ffn_gate_b, L2_ffn_up_a, L2_ffn_up_b, L2_ffn_down_a, L2_ffn_down_b)
    x = x + jnp.tanh(g_xattn[3]) * _L3_xattn_ref(_layernorm(x, axis=-1), ctx_4096, L3_xattn_Wq, L3_xattn_Wk, L3_xattn_Wv, L3_xattn_Wo)
    x = x + jnp.tanh(g_ffn[3]) * _L3_ffn_ref(_layernorm(x, axis=-1), L3_ffn_qweight, L3_ffn_weight_scale, L3_ffn_weight_zero_point, L3_ffn_bias)
    return x

_drawn_inputs = setup_inputs


def setup_inputs(seed=0):
    import zlib

    import numpy as np

    out = dict(_drawn_inputs(seed))
    spreads = {'L0_ffn_br': (0.0, 0.72),
     'L1_xattn_ln_weight': (1.0, 0.2),
     'L2_xattn_q_norm_w': (1.0, 0.2),
     'L2_xattn_k_norm_w': (1.0, 0.2)}
    factors = {'L2_ffn_gate_a': 8.0,
     'L2_ffn_gate_b': 8.0,
     'L2_ffn_up_a': 8.0,
     'L2_ffn_up_b': 8.0,
     'L2_ffn_down_a': 8.0,
     'L2_ffn_down_b': 8.0,
     'L3_ffn_weight_zero_point': 8.0}
    for name, (base, spread) in spreads.items():
        noise = np.random.default_rng([zlib.crc32(name.encode()), seed]).standard_normal(out[name].shape)
        drawn = base * np.exp(spread * noise) if base else spread * noise
        out[name] = jnp.asarray(drawn.astype(out[name].dtype))
    for name, factor in factors.items():
        out[name] = (out[name] * factor).astype(out[name].dtype)
    return out
```

```python
from contextlib import ExitStack

import numpy as np

import concourse.bass as bass
from concourse import mybir

F32 = mybir.dt.float32
F32R = mybir.dt.float32r
I32 = mybir.dt.int32
U8 = mybir.dt.uint8
U32 = mybir.dt.uint32
ALU = mybir.AluOpType
ACT = mybir.ActivationFunctionType
AX_X = mybir.AxisListType.X

P = 128
B = 8
D = 512
KT = D // P
TOK = B * P
HALF = TOK // 2
HEADS = 32
EPS = 1e-5
RAW = 2
RING = 8
HIDDEN_TILES = 11
MASKED = 1e30


class Attention:

    def __init__(self, name, heads, units, period):
        self.name = name
        self.heads = heads
        self.U = units
        self.NU = heads * units
        self.period = period
        self.nb = 1 if name == "L0" else B // units
        self.key_tiles = 2 if name == "L3" else 1
        self.group = 4
        self.piece = {}
        self.tile = {}
        self.rstd = {}
        self.evac = {}
        self.order = []
        self.prologue()
        for i in range(self.NU + 2):
            for what in self.pieces(i):
                self.count_piece(what)
            if self.has_O(i):
                for b in self.out_batches(i - 2):
                    self.tile[(i - 2, b)] = len(self.tile) + 1
                if (i - 2) % self.U == self.U - 1:
                    self.order.append(("o", (i - 2) // self.U))
            for what in self.value_pieces(i):
                self.count_piece(what)
        self.chunk = {c: n for n, c in enumerate(self.order)}

    def count_piece(self, what):
        kind, h, part = what
        self.piece[what] = len(self.piece) + 1
        if kind != "K":
            self.evac[what] = len(self.evac) + 1
        if kind in ("q", "K") and self.name == "L2":
            self.rstd[what] = len(self.rstd) + 1
        if kind in ("q", "k") and part == 1:
            self.order.append((kind, h))
        if kind == "v" and part == B - 1:
            self.order += [("v", h, kt) for kt in range(KT)]

    def prologue(self):
        both, tiles = range(2), range(B)
        norm = [("ln", 0, b) for b in tiles]
        q = [("q", 0, t) for t in both]
        if self.name == "L0":
            self.first = [("v0", 0, t) for t in both] + [("k", 0, t) for t in both] + norm + q
        if self.name == "L1":
            self.first = [("k", 0, t) for t in both]
            self.first += [w for b in tiles for w in (("v", 0, b), norm[b])] + q
        if self.name == "L2":
            self.first = [(kind, g, b) for kind, g in (("K", 0), ("K", 1), ("V", 0)) for b in tiles]
            self.first += [w for b in tiles for w in (("V", 1, b), norm[b])] + q
        if self.name == "L3":
            self.first = [("Kc", g, t) for g in range(4) for t in both]
            self.first += [w for b in tiles for w in (("Vc", 0, b), norm[b])]
            self.first += [("Kx", g, t) for g in range(4) for t in both]
            self.first += [("Vx", 0, b) for b in tiles] + q
        for what in self.first:
            kind, h, part = what
            if kind == "ln":
                continue
            self.count_piece(what)
            if kind == "v0" and part == 1:
                self.order.append(("v0", 0))
            if kind in ("K", "V") and part == B - 1:
                self.order += [(kind, h, kt) for kt in range(KT)]
            if kind == "Kx" and part == 1:
                self.order.append(("K", h))
            if kind == "Vx" and part == B - 1:
                self.order += [("V", 0, kt) for kt in range(KT)]

    def parts(self, i):
        t = i % self.U
        if i >= self.NU or i // self.U + 1 >= self.heads:
            return []
        if self.name == "L0":
            return [("k" if t < 8 else "q", t % 8 // 4, t % 4, 1)]
        if self.name == "L1":
            return [("q", t, 0, KT), ("k", t, 0, KT)]
        if self.name == "L2":
            return [("q", t, 0, KT)]
        return [("q", t // 2, t % 2 * 2, 2)]

    def pieces(self, i):
        return [(kind, i // self.U + 1, half) for kind, half, kt, n in self.parts(i) if kt + n == KT]

    def value_pieces(self, i):
        if self.name != "L1":
            return []
        period = self.group * self.U
        if i % period == period - 1 and i < self.NU - 1:
            return [("v", i // period + 1, b) for b in range(B // 2)]
        if i % period == 0 and 0 < i < self.NU:
            return [("v", i // period, b) for b in range(B // 2, B)]
        return []

    def batches(self, i):
        if self.name == "L0":
            return [i % self.U // 2]
        t = i % self.U
        return list(range(t * self.nb, (t + 1) * self.nb))

    def has_O(self, i):
        return i >= 2 and (self.name != "L0" or i % 2 == 1)

    def out_batches(self, i):
        return self.batches(i)

    def lead(self):
        if not self.period:
            return self.NU + 2, 0
        lead = 10 if self.name == "L1" else 2
        return lead, (self.NU - lead) // self.period


def at(layer, f, k, it):
    if it is None:
        return f(k)
    grows = f(k + layer.period) - f(k)
    assert all(f(k + n * layer.period) == f(k) + n * grows for n in range(layer.lead()[1]))
    return f(k) + it * grows


def run_steps(engine, layer, step):
    lead, iterations = layer.lead()
    for k in range(lead):
        step(k, None)
    if iterations:
        with engine.Fori(0, iterations) as it:
            for k in range(lead, lead + layer.period):
                step(k, it)
    for k in range(lead + iterations * layer.period, layer.NU + 2):
        step(k, None)


ATT = [Attention("L0", 4, 16, 0), Attention("L1", HEADS, 2, 8),
       Attention("L2", HEADS, 2, 8), Attention("L3", HEADS, 4, 32)]
MLP_ORDER = {
    0: [("R",), ("A",), ("B",)],
    1: [("R",), ("A",)] + [("W", kt) for kt in range(KT)] + [("B",)],
    2: [("A",), ("g", 0), ("u", 0)] + [c for j in range(HIDDEN_TILES) for c in
                                       ([("g", j + 1), ("u", j + 1)] if j + 1 < HIDDEN_TILES else [])
                                       + [("l", j), ("d", j)]] + [("b",)],
    3: [],
}


def stream_order():
    out = []
    for n in range(4):
        out += [(f"L{n}", c) for c in ATT[n].order]
        out += [(f"F{n}", c) for c in MLP_ORDER[n]]
    return out


STREAM = stream_order()
CHUNK_AT = {c: n for n, c in enumerate(STREAM)}
STREAM_LEN = -(-len(STREAM) // RING) * RING


def build(nc, x_in, ctx_t, mask, mask_add, gates, stream, lora_bias, position_bias, ln_weight,
          qk_norm, qweight, q_scale, q_zero, q_bias, out):
    ctx = ExitStack()
    with ctx:
        def sb(name, shape, dt=F32, stack=ctx):
            return stack.enter_context(nc.sbuf_tensor(name, shape, dt))

        def sem(name):
            return ctx.enter_context(nc.semaphore(name))

        x = sb("x", [P, B, D])
        xt_hi = sb("xt_hi", [P, KT, TOK], F32R)
        xt_lo = sb("xt_lo", [P, KT, TOK], F32R)
        ct_hi = sb("ct_hi", [P, KT, TOK], F32R)
        ct_lo = sb("ct_lo", [P, KT, TOK], F32R)
        w_hi = sb("w_hi", [P, RING, D], F32R)
        w_lo = sb("w_lo", [P, RING, D], F32R)
        raw = sb("raw", [P, RAW, D])
        probs = sb("probs", [P, 2, D])
        ident = sb("ident", [P, P])
        ones = sb("ones", [P, 2])
        zero = sb("zero", [P, 1])
        gate = sb("gate", [P, 8])
        stats = sb("stats", [P, B, 6])
        mv = sb("mv", [P, B, 2])
        rstd = sb("rstd", [P, B])
        nt = sb("nt", [P, 3, B])
        top = sb("top", [P, 2, 4])
        sums = sb("sums", [P, 2, 4])
        inv = sb("inv", [P, 2, 4])

        def attention_buffers(stack, n):
            return {
                "qT": sb(f"qT{n}", [P, 2, TOK], F32, stack),
                "pT": sb(f"pT{n}", [P, D], F32, stack),
                "a_hi": sb(f"a_hi{n}", [P, D], F32R, stack),
                "a_lo": sb(f"a_lo{n}", [P, D], F32R, stack),
            }

        with ExitStack() as st:
            A0 = attention_buffers(st, 0)
            A0["kT"] = sb("kT0", [P, 2, TOK], F32, st)
            A0["vT"] = sb("vT0", [P, TOK], F32, st)
            A0["v"] = sb("v0", [P, B, P], F32, st)
            A0["kz"] = sb("kz", [P, 2, D], F32, st)
            A0["vz"] = sb("vz", [P, 2, 240], F32, st)
            A0["bd"] = sb("bd", [P, 2, 4], F32, st)
            A0["ctx_raw"] = sb("ctx_raw", [P, 2, TOK], F32, st)
        with ExitStack() as st:
            A1 = attention_buffers(st, 1)
            A1["kT"] = sb("kT1", [P, 2, TOK], F32, st)
            A1["v"] = sb("v1", [P, B, D], F32, st)
            A1["ln_w"] = sb("ln_w", [P, D], F32, st)
            A1["m8"] = sb("m8", [P, B, P // 4], U32, st)
            A1["m"] = sb("m", [P, B, P], F32, st)
            A1["pb"] = sb("pb", [P, HEADS, P], F32, st)
            A1["r2"] = sb("r2", [P, B], F32, st)
            A1["sq"] = sb("sq1", [P, D], F32, st)
        with ExitStack() as st:
            A2 = attention_buffers(st, 2)
            A2["kT"] = sb("kT2", [P, 8, TOK], F32, st)
            A2["v"] = sb("v2", [P, B, 2 * D], F32, st)
            A2["vc"] = sb("vc2", [P, B, P], F32, st)
            A2["sq"] = sb("sq2", [P, D], F32, st)
            A2["madd"] = sb("madd", [P, P], F32, st)
            A2["rq"] = sb("rq", [P, 4, 4], F32, st)
            A2["rk"] = sb("rk", [P, 2, 4], F32, st)
            A2["qk_w"] = sb("qk_w", [P, 2], F32, st)
        with ExitStack() as st:
            A3 = attention_buffers(st, 3)
            A3["kT"] = sb("kT3", [P, 4, B, 2 * P], F32, st)
            A3["v"] = sb("v3", [P, 2, B, D], F32, st)
            A3["vc"] = sb("vc3", [P, 2, B, P], F32, st)
        BUF = [A0, A1, A2, A3]

        def mixture_buffers(n):
            with ExitStack() as st:
                return {
                    "lgT": sb(f"lgT{n}", [P, TOK], F32, st), "lowT": sb(f"lowT{n}", [P, TOK], F32, st),
                    "pr": sb(f"pr{n}", [P, B, 8], F32, st), "pw": sb(f"pw{n}", [P, B, 8], F32, st),
                    "s1": sb(f"s1{n}", [P, B, 8], F32, st), "s2": sb(f"s2{n}", [P, B, 8], F32, st),
                    "ex": sb(f"ex{n}", [P, 8], F32, st), "red": sb(f"red{n}", [P, 2, B], F32, st),
                    "sx": sb(f"sx{n}", [P, B, P], F32, st), "hm": sb(f"hm{n}", [P, TOK], F32, st),
                    "h_hi": sb(f"h_hi{n}", [P, TOK], F32R, st), "h_lo": sb(f"h_lo{n}", [P, TOK], F32R, st),
                }

        MIX = {0: mixture_buffers(0), 1: mixture_buffers(1)}
        with ExitStack() as st:
            M2 = {
                "low_hi": sb("low_hi", [P, TOK], F32R, st), "low_lo": sb("low_lo", [P, TOK], F32R, st),
                "sg": sb("sg", [P, 2, HALF], F32, st), "hid": sb("hid", [P, 2, HALF], F32, st),
                "h_hi": sb("hid_hi", [P, 2, TOK], F32R, st), "h_lo": sb("hid_lo", [P, 2, TOK], F32R, st),
                "dl_hi": sb("dl_hi", [P, TOK], F32R, st), "dl_lo": sb("dl_lo", [P, TOK], F32R, st),
            }
        with ExitStack() as st:
            M3 = {
                "qw": sb("qw", [P, KT, 384], I32, st), "u": sb("u", [P, KT, D], I32, st),
                "wn": sb("wn", [P, KT, D], F32, st), "sc": sb("q_sc", [P, KT], F32, st),
                "zp": sb("q_zp", [P, KT], F32, st), "bias": sb("q_bi", [P, D], F32, st),
                "wT_hi": sb("wT_hi", [P, KT, D], F32R, st), "wT_lo": sb("wT_lo", [P, KT, D], F32R, st),
            }

        def bank(name):
            return ctx.enter_context(nc.psum_tensor(name, [P, D], F32))

        J = [bank("proj0"), bank("proj1")]
        S = [bank("score0"), bank("score1")]
        T = bank("turned")
        V = bank("value")
        O = [bank("outp0"), bank("outp1")]
        TV = [T, V]

        raw_in = [sem(f"raw_in{k}") for k in range(RAW)]
        w_hi_done = sem("w_hi_done")
        w_done = sem("w_done")
        w_free = sem("w_free")
        x_in_s = [sem("x_in0"), sem("x_in1")]
        gate_in, pb_in = sem("gate_in"), sem("pb_in")
        ctx_in = [sem("ctx_in0"), sem("ctx_in1")]
        phase_in = {n: sem(f"phase_in{n}") for n in ("F0", "L1", "L2", "F3")}
        setup_done = sem("setup_done")
        gate_done = sem("gate_done")
        ctx_hi_done, ctx_done = sem("ctx_hi_done"), sem("ctx_done")
        stored = sem("stored")
        ln_rows = sem("ln_rows")
        ln_turned = sem("ln_turned")
        ln_hi, ln_lo = sem("ln_hi"), sem("ln_lo")
        ln_tiny = sem("ln_tiny")
        ln_sq, ln_y = sem("ln_sq"), sem("ln_y")

        def sems(suffix, names):
            return {name: sem(name + suffix) for name in names.split()}

        common = "scores turned values proj outp j_out exp pT a_hi top inv probs a_lo x_acc"
        AS = [
            sems("_L0", common + " kz vz vt v_rows"),
            sems("_L1", common + " seen masked clamp sum m_ready r2 added"),
            sems("_L2", common + " seen vc qss sq ksum newton rms k_turned k_out wqk"),
            sems("_L3", common + " vc"),
        ]
        FS = [
            sems("_F0", "proj low l_turned probs s_exp sx s_turned hm h_hi h_lo outp x_acc tiny"),
            sems("_F1", "proj low l_turned probs s_exp sx s_turned hm h_hi h_lo outp x_acc tiny"),
            sems("_F2", "proj low_hi low_lo silu hid h_hi h_lo dl dl_hi dl_lo outp x_acc"),
            sems("_F3", "codes wn w_turned wT_hi wT_lo outp x_acc"),
        ]

        block = ctx.enter_context(nc.Block())
        SETUP = 8
        LN2 = 2

        ADDS = []
        for n in range(4):
            ADDS.append((AS[n]["x_acc"], len(ATT[n].tile)))
            ADDS.append((FS[n]["x_acc"], {0: B, 1: 2 * B, 2: (HIDDEN_TILES + 1) * B, 3: 2 * B}[n]))

        def phase_start(eng, n):
            if n:
                eng.wait_ge(*ADDS[n - 1])

        def f32(ap):
            return ap.bitcast(F32)

        def tokens(b):
            return slice(b * P, (b + 1) * P)

        def half(t):
            return slice(t * HALF, (t + 1) * HALF)

        def chunk_no(layer, what):
            return CHUNK_AT[(layer.name, what)]

        @block.sync
        def _(sp):
            for k in range(RAW):
                sp.dma_start(raw[:, k, :], stream[k]).then_inc(raw_in[k], 16)
            with sp.Fori(0, STREAM_LEN // RAW - 1) as it:
                for k in range(RAW):
                    sp.wait_ge(w_done, it * RAW + (k + 1))
                    sp.dma_start(raw[:, k, :], stream[it * RAW + (RAW + k)]).then_inc(raw_in[k], 16)
            for b in range(B):
                sp.wait_ge(FS[3]["x_acc"], 2 * b + 2)
                sp.dma_start(out[b], x[:, b, :]).then_inc(stored, 16)
            sp.wait_ge(stored, 16 * B)

        @block.gpsimd
        def _(pool):
            bd = A0["bd"]
            pool.memset(ident[:, :], 0.0).then_inc(setup_done, 1)
            pool.memset(A0["vz"][:, :, :], 0.0).then_inc(setup_done, 1)
            pool.memset(bd[:, :, :], 1.0).then_inc(setup_done, 1)
            pool.memset(ones[:, :], 1.0).then_inc(setup_done, 1)
            pool.memset(zero[:, :], 0.0).then_inc(setup_done, 1)
            pool.wait_ge(setup_done, 5)
            pool.affine_select(out=ident[:, :], in_=ident[:, :], compare_op=ALU.not_equal, fill=1.0,
                               base=0, pattern=[[-1, P]], channel_multiplier=1).then_inc(setup_done, 1)
            pool.affine_select(out=bd[:, :, :], in_=bd[:, :, :], compare_op=ALU.is_ge, fill=0.0,
                               base=0, pattern=[[-64, 2], [-16, 4]], channel_multiplier=1)\
                .then_inc(setup_done, 1)
            pool.wait_ge(setup_done, 7)
            pool.affine_select(out=bd[:, :, :], in_=bd[:, :, :], compare_op=ALU.is_ge, fill=0.0,
                               base=15, pattern=[[64, 2], [16, 4]], channel_multiplier=-1)\
                .then_inc(setup_done, 1)

            def split(k, chunk_raw, chunk_hi):
                pool.wait_ge(raw_in[k % RAW], chunk_raw)
                pool.tensor_tensor(w_hi[:, k, :], raw[:, k % RAW, :], zero[:, :].to_broadcast([P, D]),
                                   ALU.add)\
                    .then_inc(w_hi_done, 1)
                pool.wait_ge(w_hi_done, chunk_hi)
                pool.tensor_tensor(w_lo[:, k, :], raw[:, k % RAW, :], f32(w_hi[:, k, :]), ALU.subtract)\
                    .then_inc(w_done, 1)

            for k in range(RING):
                split(k, 16 * (k // RAW + 1), k + 1)
            with pool.Fori(0, STREAM_LEN // RING - 1) as it:
                for k in range(RING):
                    pool.wait_ge(w_free, it * RING + (k + 1))
                    split(k, it * (16 * RING // RAW) + 16 * ((RING + k) // RAW + 1), it * RING + (RING + k + 1))

        @block.tensor
        def _(pe):
            owed = [0]

            def mm(out_, l, r, start, stop):
                m = pe.matmul(out_, l, r, start=start, stop=stop, skip_group_check=True)
                return m

            def told(m):
                if owed[0]:
                    m.then_inc(w_free, 1)
                    owed[0] -= 1
                return m

            def mm3(out_, l, r, start, stop, last=False):
                for n, (a, b) in enumerate(((1, 0), (0, 1), (0, 0))):
                    m = mm(out_, l[a], r[b], start and n == 0, stop and n == 2)
                    if not (last and n == 2):
                        told(m)
                return m

            def ring(c, cols=slice(0, D)):
                s = c % RING
                return w_hi[:, s, cols], w_lo[:, s, cols]

            def acts(which, kt, cols):
                hi, lo = (xt_hi, xt_lo) if which == "x" else (ct_hi, ct_lo)
                return hi[:, kt, cols], lo[:, kt, cols]

            def by_feature(dst, c, which, t, kts=range(KT), last=False):
                for kt in kts:
                    m = mm3(dst, ring(c, tokens(kt)), acts(which, kt, half(t)),
                            kt == 0, kt == KT - 1, last and kt == kts[-1])
                return m

            def by_token(dst, cs, which, b, last=False):
                for kt in range(KT):
                    m = mm3(dst, acts(which, kt, tokens(b)), ring(cs[kt]),
                            kt == 0, kt == KT - 1, last and kt == KT - 1)
                return m

            def norm_tile(n, b):
                pe.wait_ge(ln_y if n == 2 else ln_rows, b + 1 if n == 2 else B * n + b + 1)
                if b >= 2:
                    pe.wait_ge(ln_hi, B * n + b - 1)
                    pe.wait_ge(ln_lo, B * n + b - 1)
                for kt in range(KT):
                    m = pe.transpose(TV[b % 2][:, tokens(kt)], probs[:, b % 2, tokens(kt)], ident[:, :])
                m.then_inc(ln_turned, 1)

            def wait_norm(n, tiles):
                pe.wait_ge(ln_hi, B * n + tiles)
                pe.wait_ge(ln_lo, B * n + tiles)

            def attention(n):
                L, s, buf = ATT[n], AS[n], BUF[n]
                name = L.name
                phase_start(pe, 2 * n)
                if n == 0:
                    pe.wait_ge(setup_done, SETUP)
                    pe.wait_ge(ctx_hi_done, KT)
                    pe.wait_ge(ctx_done, KT)
                by_no = {v: k for k, v in L.piece.items()}

                def bank_free(what_f, k, it):
                    no = L.piece[what_f(k)]
                    if no <= 2:
                        return
                    before = by_no[no - 2]
                    if before in L.rstd:
                        def f(i):
                            return L.rstd[by_no[L.piece[what_f(i)] - 2]]
                        pe.wait_ge(s["rms"], at(L, f, k, it))
                    else:
                        pe.wait_ge(s["j_out"], at(L, lambda i: L.evac[by_no[L.piece[what_f(i)] - 2]], k, it))

                def chunk(what_f, k, it):
                    pe.wait_ge(w_done, at(L, lambda i: chunk_no(L, what_f(i)) + 1, k, it))
                    return chunk_no(L, what_f(k))

                def chunks(what_f, k, it):
                    chunk(lambda i: (*what_f(i), KT - 1), k, it)
                    return [chunk_no(L, (*what_f(k), kt)) for kt in range(KT)]

                def dst(what):
                    return J[L.piece[what] % 2][:, :]

                def first_piece(what):
                    kind, h, part = what
                    bank_free(lambda i: what, 0, None)
                    which = "x" if kind in ("q", "Kx", "Vx") else "c"
                    if which == "x":
                        wait_norm(2 * n, part + 1 if kind == "Vx" else (part + 1) * (B // 2))
                    if kind in ("K", "V", "v", "Vc", "Vx"):
                        c = chunks(lambda i: (kind[0], h), 0, None)
                        by_token(dst(what), c, which, part, last=True).then_inc(s["proj"], 1)
                        if part == B - 1 and kind != "Vc":
                            owed[0] += KT
                    else:
                        c = chunk(lambda i: ((kind if kind == "v0" else kind[0]), h), 0, None)
                        by_feature(dst(what), c, which, part, last=True).then_inc(s["proj"], 1)
                        if part == 1 and kind != "Kc":
                            owed[0] += 1

                def q_squares(what_f, k, it):
                    pe.wait_ge(s["sq"], at(L, lambda i: L.rstd[what_f(i)], k, it))
                    bank_ = dst(what_f(k))
                    for j in range(4):
                        m = mm(bank_[:, 2 * j:2 * j + 2], buf["sq"][:, tokens(j)], ones[:, :], True, True)
                    m.then_inc(s["qss"], 1)

                def turn_keys(what):
                    _, g, b = what
                    no = g * B + b
                    pe.wait_ge(s["rms"], no + 1)
                    if no >= 2:
                        pe.wait_ge(s["k_out"], no - 1)
                    for j in range(4):
                        m = pe.transpose(TV[b % 2][:, tokens(j)], probs[:, b % 2, tokens(j)], ident[:, :])
                    m.then_inc(s["k_turned"], 1)

                behind = None
                for what in L.first:
                    if what[0] == "ln":
                        if n == 0 and what[2] == 0:
                            pe.wait_ge(s["v_rows"], 2)
                        if n == 2 and what[2] == 0:
                            pe.wait_ge(s["k_out"], 2 * B)
                        norm_tile(2 * n, what[2])
                        continue
                    first_piece(what)
                    if n == 2 and behind:
                        turn_keys(behind)
                    behind = what if what[0] == "K" else None
                    if n == 2 and what[0] == "q":
                        q_squares(lambda i: what, 0, None)
                    if what == ("v0", 0, 1):
                        pe.wait_ge(s["j_out"], 2)
                        for b in range(B):
                            m = pe.transpose(TV[b // 4][:, tokens(b % 4)], buf["vT"][:, tokens(b)], ident[:, :])
                        m.then_inc(s["vt"], 1)

                def scores(k, it):
                    h, t = k // L.U, k % L.U
                    kinds = "qk" if n == 1 else "q"
                    pe.wait_ge(s["j_out"], at(L, lambda i: max(
                        L.evac[(kind, i // L.U, L.batches(i)[0] // (B // 2))] for kind in kinds), k, it))
                    if k >= 2:
                        pe.wait_ge(s["seen"] if n in (1, 2) else s["exp"], at(L, lambda i: i - 1, k, it))
                    bank_ = S[k % 2]
                    qT = buf["qT"][:, h % 2, :]
                    if n == 0:
                        pe.wait_ge(s["kz"], k + 1)
                        b = L.batches(k)[0]
                        mm(bank_[:, :], qT[:, tokens(b)], buf["kz"][:, k % 2, :], True, True)\
                            .then_inc(s["scores"], 1)
                        return
                    for j, b in enumerate(L.batches(k)):
                        if n == 1:
                            keys = buf["kT"][:, h % 2, tokens(b)]
                        elif n == 2:
                            kv = at(L, lambda i: i // L.U // 4, k, it)
                            keys = buf["kT"][:, kv, tokens(b)] if it is None else \
                                buf["kT"][:, bass.ds(kv, 1), tokens(b)].rearrange("p a k -> p (a k)")
                        else:
                            kv = at(L, lambda i: i // L.U // 8, k, it)
                            keys = buf["kT"][:, kv, b, :] if it is None else \
                                buf["kT"][:, bass.ds(kv, 1), b, :].rearrange("p a k -> p (a k)")
                        w = D // len(L.batches(k))
                        m = mm(bank_[:, j * w:(j + 1) * w], qT[:, tokens(b)], keys, True, True)
                        if b != L.batches(k)[-1]:
                            told(m)
                    m.then_inc(s["scores"], 1)

                def turn(k, it):
                    pe.wait_ge(s["probs"], at(L, lambda i: i + 1, k, it))
                    if k >= 1:
                        pe.wait_ge(s["pT"], at(L, lambda i: i, k, it))
                    for j in range(4):
                        m = pe.transpose(T[:, tokens(j)], probs[:, k % 2, tokens(j)], ident[:, :])
                        if j < 3:
                            told(m)
                    m.then_inc(s["turned"], 1)

                def values(k, it):
                    pe.wait_ge(s["pT"], at(L, lambda i: i + 1, k, it))
                    if n == 0:
                        b, hf = L.batches(k)[0], k % 2
                        pe.wait_ge(s["vz"], k + 1)
                        pair = k // 2
                        if hf == 0 and pair >= 2:
                            pe.wait_ge(s["a_lo"], pair - 1)
                        for e in range(4):
                            lo = 112 - 16 * (4 * hf + e)
                            m = mm(V[:, tokens(pair % 2)], buf["vz"][:, k % 2, lo:lo + P],
                                   buf["pT"][:, tokens(e)], hf == 0 and e == 0, hf == 1 and e == 3)
                            if e < 3:
                                told(m)
                        m.then_inc(s["values"], 1)
                        return
                    if k >= 1:
                        pe.wait_ge(s["a_hi"], at(L, lambda i: i, k, it))
                        pe.wait_ge(s["a_lo"], at(L, lambda i: i, k, it))
                    h = k // L.U
                    if n == 1:
                        pe.wait_ge(s["j_out"], at(L, lambda i: L.evac[("v", i // L.U // 4, max(L.batches(i)))],
                                               k, it))
                    else:
                        per = 4 if n == 2 else 8
                        pe.wait_ge(s["vc"], at(L, lambda i: i // L.U // per + 1, k, it))
                    for j, b in enumerate(L.batches(k)):
                        for kt in range(L.key_tiles):
                            if n == 1:
                                v = buf["v"][:, b, tokens(h % 4)]
                            elif n == 2:
                                v = buf["vc"][:, b, :]
                            else:
                                v = buf["vc"][:, kt, b, :]
                            m = mm(V[:, tokens(j)], v, buf["pT"][:, tokens(j * L.key_tiles + kt)],
                                   kt == 0, kt == L.key_tiles - 1)
                            if not (b == L.batches(k)[-1] and kt == L.key_tiles - 1):
                                told(m)
                    m.then_inc(s["values"], 1)

                def output(k, it):
                    c = chunk(lambda i: ("o", (i - 2) // L.U), k + 2, it)
                    f = (lambda i: (i - 2) // 2 + 1) if n == 0 else (lambda i: i - 1)
                    pe.wait_ge(s["a_hi"], at(L, f, k + 2, it))
                    pe.wait_ge(s["a_lo"], at(L, f, k + 2, it))
                    for j, b in enumerate(L.out_batches(k)):
                        no = L.tile[(k, b)]
                        if no > 2:
                            pe.wait_ge(s["x_acc"], at(L, lambda i: L.tile[(i - 2, L.out_batches(i - 2)[j])] - 2,
                                                   k + 2, it))
                        a = buf["a_hi"][:, tokens(j)], buf["a_lo"][:, tokens(j)]
                        mm3(O[no % 2][:, :], a, ring(c), True, True, last=True).then_inc(s["outp"], 1)
                    if k % L.U == L.U - 1:
                        owed[0] += 1

                def step(k, it):
                    if k < L.NU:
                        scores(k, it)
                    if 1 <= k <= L.NU:
                        turn(k - 1, it)
                    for kind, hf, kt, kts in L.parts(k):
                        def what_f(i, kind=kind, hf=hf):
                            return (kind, i // L.U + 1, hf)
                        what = what_f(k)
                        done = kt + kts == KT
                        c = chunk(lambda i: what_f(i)[:2], k, it)
                        if kt == 0:
                            bank_free(what_f, k, it)
                        m = by_feature(dst(what), c, "x" if kind == "q" else "c", hf,
                                       range(kt, kt + kts), last=done)
                        if done:
                            m.then_inc(s["proj"], 1)
                            if hf == 1:
                                owed[0] += 1
                    if L.has_O(k):
                        output(k - 2, it)
                    if n == 2:
                        for what in L.pieces(k):
                            q_squares(lambda i: L.pieces(i)[0], k, it)
                    if 1 <= k <= L.NU:
                        values(k - 1, it)
                    for j, what in enumerate(L.value_pieces(k)):
                        def what_f(i, j=j):
                            return L.value_pieces(i)[j]
                        bank_free(what_f, k, it)
                        c = chunks(lambda i: what_f(i)[:2], k, it)
                        by_token(dst(what), c, "c", what[2], last=True).then_inc(s["proj"], 1)
                        if what[2] == B - 1:
                            owed[0] += KT

                run_steps(pe, L, step)

            def f_chunk(n, c):
                no = CHUNK_AT[(f"F{n}", c)]
                pe.wait_ge(w_done, no + 1)
                return no

            def all_norm_tiles(n):
                for b in range(B):
                    norm_tile(n, b)

            def mixture(n):
                s, buf, norm = FS[n], MIX[n], 2 * n + 1
                phase_start(pe, norm)
                all_norm_tiles(norm)
                for no, (what, t) in enumerate((w, t) for w in ("R", "A") for t in range(2)):
                    c = f_chunk(n, (what,))
                    wait_norm(norm, (t + 1) * (B // 2))
                    by_feature((J + S)[no][:, :], c, "x", t, last=True).then_inc(s["proj"], 1)
                    owed[0] += t
                pe.wait_ge(s["low"], 2)
                for b in range(B):
                    m = pe.transpose(T[:, 8 * b:8 * b + 8], buf["lgT"][0:8, tokens(b)], ident[0:8, 0:8])
                m.then_inc(s["l_turned"], 1)
                outs = 0
                if n == 1:
                    cs = [f_chunk(1, ("W", kt)) for kt in range(KT)]
                    for b in range(B):
                        if b >= 2:
                            pe.wait_ge(s["x_acc"], b - 1)
                        by_token(O[b % 2][:, :], cs, "x", b, last=True).then_inc(s["outp"], 1)
                    owed[0] += KT
                    outs = B
                pe.wait_ge(s["sx"], 1)
                for t in range(2):
                    for j in range(4):
                        m = pe.transpose(TV[t][:, tokens(j)], buf["sx"][:, 4 * t + j, :], ident[:, :])
                        if j < 3:
                            told(m)
                    m.then_inc(s["s_turned"], 1)
                c = f_chunk(n, ("B",))
                for b in range(B):
                    pe.wait_ge(s["h_hi"], b // 4 + 1)
                    pe.wait_ge(s["h_lo"], b // 4 + 1)
                    if outs + b >= 2:
                        pe.wait_ge(s["x_acc"], outs + b - 1)
                    h = buf["h_hi"][:, tokens(b)], buf["h_lo"][:, tokens(b)]
                    mm3(O[b % 2][:, :], h, ring(c), True, True, last=True).then_inc(s["outp"], 1)
                owed[0] += 1

            def swiglu():
                s, norm = FS[2], 5
                phase_start(pe, norm)
                all_norm_tiles(norm)
                c = f_chunk(2, ("A",))
                for t in range(2):
                    wait_norm(norm, (t + 1) * (B // 2))
                    by_feature(J[t][:, :], c, "x", t, last=True).then_inc(s["proj"], 1)
                owed[0] += 1
                for j in range(HIDDEN_TILES + 1):
                    if j < HIDDEN_TILES:
                        g, u, lora = (f_chunk(2, (w, j)) for w in "gul")
                        for t in range(2):
                            no = 2 * j + t
                            if no >= 2:
                                pe.wait_ge(s["hid"], no - 1)
                            if j == 0:
                                pe.wait_ge(s["low_hi"], 2)
                                pe.wait_ge(s["low_lo"], 2)
                            for w, (c, dst) in enumerate(((g, J[0] if t == 0 else S[0]),
                                                          (u, J[1] if t == 0 else S[1]))):
                                low = M2["low_hi"][:, half(t)], M2["low_lo"][:, half(t)]
                                mm3(dst[:, :], ring(lora, tokens(w)), low, True, False)
                                for kt in range(KT):
                                    last = kt == KT - 1
                                    m = mm3(dst[:, :], ring(c, tokens(kt)), acts("x", kt, half(t)),
                                            False, last, last)
                                m.then_inc(s["proj"], 1)
                                owed[0] += t
                    if j == 0:
                        continue
                    jj = j - 1
                    lora, d = f_chunk(2, ("l", jj)), f_chunk(2, ("d", jj))
                    for t in range(2):
                        pe.wait_ge(s["h_hi"], 2 * jj + t + 1)
                        pe.wait_ge(s["h_lo"], 2 * jj + t + 1)
                        h = M2["h_hi"][:, jj % 2, half(t)], M2["h_lo"][:, jj % 2, half(t)]
                        last = jj == HIDDEN_TILES - 1
                        m = mm3(TV[t][:, :], ring(lora, tokens(2)), h, jj == 0, last, last)
                        if last:
                            m.then_inc(s["dl"], 1)
                        owed[0] += t
                    for b in range(B):
                        no = jj * B + b + 1
                        if no > 2:
                            pe.wait_ge(s["x_acc"], no - 2)
                        h = M2["h_hi"][:, jj % 2, tokens(b)], M2["h_lo"][:, jj % 2, tokens(b)]
                        mm3(O[b % 2][:, :], h, ring(d), True, True, last=True).then_inc(s["outp"], 1)
                    owed[0] += 1
                c = f_chunk(2, ("b",))
                for b in range(B):
                    pe.wait_ge(s["dl_hi"], b // 4 + 1)
                    pe.wait_ge(s["dl_lo"], b // 4 + 1)
                    pe.wait_ge(s["x_acc"], HIDDEN_TILES * B + b - 1)
                    dl = M2["dl_hi"][:, tokens(b)], M2["dl_lo"][:, tokens(b)]
                    mm3(O[b % 2][:, :], dl, ring(c), True, True, last=True).then_inc(s["outp"], 1)
                owed[0] += 1

            def quantised():
                s, norm = FS[3], 7
                phase_start(pe, norm)
                pe.wait_ge(s["wn"], 4)
                for kt in range(KT):
                    for nt in range(KT):
                        m = pe.transpose((J + S)[kt][:, tokens(nt)], M3["wn"][:, nt, tokens(kt)], ident[:, :])
                    m.then_inc(s["w_turned"], 1)
                all_norm_tiles(norm)
                pe.wait_ge(s["wT_hi"], KT)
                pe.wait_ge(s["wT_lo"], KT)
                for b in range(B):
                    wait_norm(norm, b + 1)
                    if b >= 2:
                        pe.wait_ge(s["x_acc"], 2 * (b - 1))
                    for kt in range(KT):
                        m = mm3(O[b % 2][:, :], acts("x", kt, tokens(b)),
                                (M3["wT_hi"][:, kt, :], M3["wT_lo"][:, kt, :]),
                                kt == 0, kt == KT - 1, kt == KT - 1)
                    m.then_inc(s["outp"], 1)

            attention(0)
            mixture(0)
            attention(1)
            mixture(1)
            attention(2)
            swiglu()
            attention(3)
            quantised()

        @block.scalar
        def _(act):
            def copy(dst, src, scale=None):
                if scale is None:
                    return act.activation(dst, src, ACT.Copy)
                return act.activation(dst, src, ACT.Copy, scale=scale)

            def norm_hi(n, b):
                act.wait_ge(ln_turned, B * n + b + 1)
                copy(xt_hi[:, :, tokens(b)], TV[b % 2][:, :].rearrange("p (k t) -> p k t", k=KT))\
                    .then_inc(ln_hi, 1)

            def attention(n):
                L, s, buf = ATT[n], AS[n], BUF[n]
                phase_start(act, 2 * n)
                if n == 1:
                    act.dma_start(buf["m8"][:, :, :], mask).then_inc(phase_in["L1"], 16)
                    act.dma_start(buf["ln_w"][:, :], ln_weight).then_inc(phase_in["L1"], 16)
                if n == 2:
                    act.dma_start(buf["madd"][:, :], mask_add).then_inc(phase_in["L2"], 16)
                    act.dma_start(buf["qk_w"][:, :], qk_norm).then_inc(phase_in["L2"], 16)
                q_scale_ = {0: 16.0 ** -0.5, 3: float(P) ** -0.5}.get(n)

                def squares(what_f, src, k, it):
                    m = L.rstd[what_f(k)]
                    if 1 < m <= 2 * B + 1:
                        act.wait_ge(s["ksum"], m - 1)
                    elif m > 1:
                        act.wait_ge(s["qss"], at(L, lambda i: L.rstd[what_f(i)] - 1 - 2 * B, k, it))
                    act.activation(buf["sq"][:, :], src, ACT.Square).then_inc(s["sq"], 1)

                def leave_bank(what_f, k, it):
                    what = what_f(k)
                    kind, h, part = what
                    src = J[L.piece[what] % 2][:, :]
                    by_tile = src.rearrange("p (b t) -> p b t", b=4)
                    act.wait_ge(s["proj"], at(L, lambda i: L.piece[what_f(i)], k, it))
                    if kind == "K":
                        squares(what_f, src, k, it)
                        return
                    scale = None
                    if kind == "q":
                        dst, scale = buf["qT"][:, h % 2, half(part)], q_scale_
                    elif kind == "k":
                        dst = buf["kT"][:, h % 2, half(part)]
                    elif kind == "v0":
                        dst = buf["vT"][:, half(part)]
                    elif kind == "v":
                        dst = buf["v"][:, part, :]
                    elif kind == "V":
                        dst = buf["v"][:, part, h * D:(h + 1) * D]
                    elif kind in ("Kc", "Kx"):
                        o = 0 if kind == "Kc" else P
                        dst, src = buf["kT"][:, h, 4 * part:4 * part + 4, o:o + P], by_tile
                    else:
                        dst = buf["v"][:, 0 if kind == "Vc" else 1, part, :]
                    copy(dst, src, scale).then_inc(s["j_out"], 1)
                    if kind == "q" and n == 2:
                        squares(what_f, J[L.piece[what] % 2][:, :], k, it)

                def keys_out(what):
                    _, g, b = what
                    act.wait_ge(s["k_turned"], g * B + b + 1)
                    act.wait_ge(s["wqk"], 1)
                    act.activation(buf["kT"][:, 4 * g:4 * g + 4, tokens(b)],
                                   TV[b % 2][:, :].rearrange("p (h t) -> p h t", h=4),
                                   ACT.Copy, scale=buf["qk_w"][:, 0:1]).then_inc(s["k_out"], 1)

                behind = None
                for what in L.first:
                    if what[0] == "ln":
                        if n == 1:
                            b = what[2]
                            act.wait_ge(ln_rows, B * LN2 + b + 1)
                            act.activation(buf["sq"][:, :], probs[:, b % 2, :], ACT.Square,
                                           accum_out=buf["r2"][:, b:b + 1]).then_inc(ln_sq, 1)
                        norm_hi(2 * n, what[2])
                        continue
                    leave_bank(lambda i: what, 0, None)
                    if n == 2 and behind:
                        keys_out(behind)
                    behind = what if what[0] == "K" else None
                    if what == ("v0", 0, 1):
                        act.wait_ge(s["vt"], 1)
                        for t in range(2):
                            copy(buf["v"][:, 4 * t:4 * t + 4, :], TV[t][:, :].rearrange("p (b t) -> p b t", b=4))\
                                .then_inc(s["v_rows"], 1)

                def step(k, it):
                    if 1 <= k <= L.NU:
                        act.wait_ge(s["turned"], at(L, lambda i: i, k, it))
                        copy(buf["pT"][:, :], T[:, :]).then_inc(s["pT"], 1)
                    if k < L.NU:
                        act.wait_ge(s["top"], at(L, lambda i: i + 1, k, it))
                        if k >= 2 and n in (0, 3):
                            act.wait_ge(s["turned"], at(L, lambda i: i - 1, k, it))
                        blocks = 2 if n == 3 else 4
                        w = D // blocks
                        src = S[k % 2] if n in (0, 3) else probs[:, k % 2, :]
                        for j in range(blocks):
                            cols = slice(j * w, (j + 1) * w)
                            e = act.activation(probs[:, k % 2, cols], src[:, cols], ACT.Exp,
                                               bias=top[:, k % 2, j:j + 1], scale=1.0,
                                               accum_out=sums[:, k % 2, j:j + 1])
                        e.then_inc(s["exp"], 1)
                    per = {2: 4 * L.U, 3: 8 * L.U}.get(n, 0)
                    if per and k % per == 1 and k < L.NU:
                        if k > 1:
                            act.wait_ge(s["values"], at(L, lambda i: i - 1, k, it))
                        kv = at(L, lambda i: i // per, k, it)
                        cols = bass.ds(kv * P, P)
                        if n == 2:
                            copy(buf["vc"][:, :, :], buf["v"][:, :, cols]).then_inc(s["vc"], 1)
                        else:
                            copy(buf["vc"][:, :, :, :].rearrange("p a b d -> p (a b) d"),
                                 buf["v"][:, :, :, :].rearrange("p a b d -> p (a b) d")[:, :, cols])\
                                .then_inc(s["vc"], 1)
                    for j in range(len(L.pieces(k))):
                        leave_bank(lambda i, j=j: L.pieces(i)[j], k, it)
                    if 1 <= k <= L.NU and not (n == 0 and k % 2 == 1):
                        act.wait_ge(s["values"], at(L, lambda i: i, k, it))
                        w = L.nb * P
                        o = (k // 2 - 1) % 2 * P if n == 0 else 0
                        copy(buf["a_hi"][:, 0:w], V[:, o:o + w]).then_inc(s["a_hi"], 1)
                    for j in range(len(L.value_pieces(k))):
                        leave_bank(lambda i, j=j: L.value_pieces(i)[j], k, it)

                run_steps(act, L, step)

            def mixture(n):
                s, buf, norm = FS[n], MIX[n], 2 * n + 1
                phase_start(act, norm)
                if n == 0:
                    act.dma_start(buf["ex"][:, :], lora_bias).then_inc(phase_in["F0"], 16)
                for b in range(B):
                    norm_hi(norm, b)
                for no in range(4):
                    act.wait_ge(s["proj"], no + 1)
                    copy(buf["lgT" if no < 2 else "lowT"][:, half(no % 2)], (J + S)[no][:, :]).then_inc(s["low"], 1)
                act.wait_ge(s["probs"], 1)
                act.activation(buf["pr"][:, :, :], buf["pr"][:, :, :], ACT.Exp).then_inc(s["s_exp"], 1)
                for t in range(2):
                    act.wait_ge(s["hm"], t + 1)
                    copy(buf["h_hi"][:, half(t)], buf["hm"][:, half(t)]).then_inc(s["h_hi"], 1)

            def swiglu():
                s, norm = FS[2], 5
                phase_start(act, norm)
                for b in range(B):
                    norm_hi(norm, b)
                for t in range(2):
                    act.wait_ge(s["proj"], t + 1)
                    copy(M2["low_hi"][:, half(t)], J[t][:, :]).then_inc(s["low_hi"], 1)
                for j in range(HIDDEN_TILES):
                    for t in range(2):
                        no = 2 * j + t
                        act.wait_ge(s["proj"], 2 + 2 * no + 1)
                        if no >= 2:
                            act.wait_ge(s["hid"], no - 1)
                        act.activation(M2["sg"][:, t, :], (J if t == 0 else S)[0][:, :], ACT.Silu)\
                            .then_inc(s["silu"], 1)
                        act.wait_ge(s["hid"], no + 1)
                        if j >= 2:
                            act.wait_ge(s["outp"], (j - 1) * B)
                        copy(M2["h_hi"][:, j % 2, half(t)], M2["hid"][:, t, :]).then_inc(s["h_hi"], 1)
                for t in range(2):
                    act.wait_ge(s["dl"], t + 1)
                    copy(M2["dl_hi"][:, half(t)], TV[t][:, :]).then_inc(s["dl_hi"], 1)

            def quantised():
                s, norm = FS[3], 7
                phase_start(act, norm)
                act.dma_start(M3["qw"][:, :, :], qweight).then_inc(phase_in["F3"], 16)
                act.dma_start(M3["sc"][:, :], q_scale).then_inc(phase_in["F3"], 16)
                act.dma_start(M3["zp"][:, :], q_zero).then_inc(phase_in["F3"], 16)
                act.dma_start(M3["bias"][:, :], q_bias).then_inc(phase_in["F3"], 16)
                for kt in range(KT):
                    act.wait_ge(s["w_turned"], kt + 1)
                    copy(M3["wT_hi"][:, kt, :], (J + S)[kt][:, :]).then_inc(s["wT_hi"], 1)
                for b in range(B):
                    norm_hi(norm, b)

            for kt in range(2):
                act.dma_start(A0["ctx_raw"][:, kt, :], ctx_t[kt]).then_inc(ctx_in[kt], 16)
            for b in range(B):
                act.dma_start(x[:, b, :], x_in[b]).then_inc(x_in_s[b % 2], 16)
            act.dma_start(gate[:, :], gates).then_inc(gate_in, 16)
            act.wait_ge(gate_in, 16)
            act.activation(gate[:, :], gate[:, :], ACT.Tanh).then_inc(gate_done, 1)
            for kt in range(KT):
                act.wait_ge(ctx_in[kt % 2], 16 * (kt // 2 + 1))
                copy(ct_hi[:, kt, :], A0["ctx_raw"][:, kt % 2, :]).then_inc(ctx_hi_done, 1)
                if kt < 2:
                    act.wait_ge(ctx_done, kt + 1)
                    act.dma_start(A0["ctx_raw"][:, kt, :], ctx_t[kt + 2]).then_inc(ctx_in[kt], 16)
            act.dma_start(A1["pb"][:, :, :], position_bias).then_inc(pb_in, 16)
            attention(0)
            mixture(0)
            attention(1)
            mixture(1)
            attention(2)
            swiglu()
            attention(3)
            quantised()

        @block.vector
        def _(dve):
            def rsqrt(v, y, t, sem_, base, final):
                no = [base]

                def then(ins):
                    no[0] = no[0] + 1
                    ins.then_inc(sem_, 1)
                    dve.wait_ge(sem_, no[0])

                then(dve.tensor_scalar(t.bitcast(I32), v.bitcast(I32), 1, None, ALU.logical_shift_right))
                then(dve.tensor_scalar(y.bitcast(I32), t.bitcast(I32), -1.0, float(0x5F3759DF), ALU.mult, ALU.add))
                for n in range(3):
                    then(dve.tensor_tensor(t, y, y, ALU.mult))
                    then(dve.scalar_tensor_tensor(out=t, in0=t, scalar=-0.5, in1=v, op0=ALU.mult, op1=ALU.mult))
                    last = dve.scalar_tensor_tensor(out=y, in0=t, scalar=1.5, in1=y, op0=ALU.add, op1=ALU.mult)
                    if n == 2 and final is not None:
                        last.then_inc(final, 1)
                    else:
                        then(last)

            LN_STEPS = 2 * B + 1 + 11

            def norm_stats(n):
                base = LN_STEPS * n
                for b in range(B):
                    if n == 0:
                        dve.wait_ge(x_in_s[b % 2], 16 * (b // 2 + 1))
                    else:
                        dve.wait_ge(ADDS[n - 1][0], ADDS[n - 1][1])
                    dve.bn_stats(stats[:, b, :], x[:, b, :]).then_inc(ln_tiny, 1)
                for b in range(B):
                    dve.wait_ge(ln_tiny, base + b + 1)
                    dve.bn_aggr(mv[:, b, :], stats[:, b, :]).then_inc(ln_tiny, 1)
                dve.wait_ge(ln_tiny, base + 2 * B)
                dve.tensor_scalar(nt[:, 0, :], mv[:, :, 1], EPS, None, ALU.add).then_inc(ln_tiny, 1)
                dve.wait_ge(ln_tiny, base + 2 * B + 1)
                rsqrt(nt[:, 0, :], rstd[:, :], nt[:, 1, :], ln_tiny, base + 2 * B + 1, None)

            def norm_rows(n, b):
                if b >= 2:
                    dve.wait_ge(ln_turned, B * n + b - 1)
                dve.tensor_scalar(probs[:, b % 2, :], x[:, b, :], mv[:, b, 0:1], rstd[:, b:b + 1],
                                  ALU.subtract, ALU.mult).then_inc(ln_rows, 1)

            def norm_lo(n, b):
                dve.wait_ge(ln_hi, B * n + b + 1)
                dve.tensor_tensor(xt_lo[:, :, tokens(b)], TV[b % 2][:, :].rearrange("p (k t) -> p k t", k=KT),
                                  f32(xt_hi[:, :, tokens(b)]), ALU.subtract).then_inc(ln_lo, 1)

            def attention(n):
                L, s, buf = ATT[n], AS[n], BUF[n]
                norm = 2 * n
                g = gate[:, n:n + 1]
                if n == 0:
                    for kt in range(KT):
                        dve.wait_ge(ctx_hi_done, kt + 1)
                        dve.tensor_tensor(ct_lo[:, kt, :], buf["ctx_raw"][:, kt % 2, :], f32(ct_hi[:, kt, :]),
                                          ALU.subtract).then_inc(ctx_done, 1)
                    dve.wait_ge(setup_done, SETUP)
                    dve.wait_ge(gate_done, 1)
                if n == 1:
                    dve.wait_ge(phase_in["L1"], 32)
                    dve.tensor_scalar(buf["m"][:, :, :], buf["m8"][:, :, :].bitcast(U8), 1.0, MASKED,
                                      ALU.subtract, ALU.mult).then_inc(s["m_ready"], 1)
                if n == 2:
                    dve.wait_ge(phase_in["L2"], 32)
                    dve.scalar_tensor_tensor(out=buf["qk_w"][:, 0:1], in0=buf["qk_w"][:, 0:1],
                                             scalar=float(P) ** 0.5, in1=buf["qk_w"][:, 1:2],
                                             op0=ALU.mult, op1=ALU.mult).then_inc(s["wqk"], 1)

                def key_rows(what):
                    _, h, b = what
                    m = L.rstd[what]
                    rk = buf["rk"][:, m % 2, :]
                    src = J[L.piece[what] % 2][:, :]
                    dve.wait_ge(s["sq"], m)
                    dve.tensor_reduce(nt[:, 2, 0:4], buf["sq"][:, :].rearrange("p (h d) -> p h d", h=4),
                                      AX_X, ALU.add).then_inc(s["ksum"], 1)
                    base = 12 * (m - 1)
                    dve.wait_ge(s["ksum"], m)
                    dve.tensor_scalar(nt[:, 0, 0:4], nt[:, 2, 0:4], P * EPS, None, ALU.add).then_inc(s["newton"], 1)
                    dve.wait_ge(s["newton"], base + 1)
                    rsqrt(nt[:, 0, 0:4], rk, nt[:, 1, 0:4], s["newton"], base + 1, None)
                    if m > 2:
                        dve.wait_ge(s["k_turned"], m - 2)
                    dve.tensor_tensor(probs[:, b % 2, :].rearrange("p (h d) -> p h d", h=4),
                                      src.rearrange("p (h d) -> p h d", h=4),
                                      rk.unsqueeze(2).to_broadcast([P, 4, P]), ALU.mult).then_inc(s["rms"], 1)

                def query_rstd(what_f, k, it):
                    _, h, part = what_f(k)
                    src = J[L.piece[what_f(k)] % 2][:, 0:8].rearrange("p (j a) -> p j a", a=2)[:, :, 0]
                    dve.wait_ge(s["qss"], at(L, lambda i: L.rstd[what_f(i)] - 2 * B, k, it))
                    base = at(L, lambda i: 12 * 2 * B + 11 * (L.rstd[what_f(i)] - 1 - 2 * B), k, it)
                    dve.tensor_scalar(nt[:, 0, 0:4], src, P * EPS, None, ALU.add).then_inc(s["newton"], 1)
                    dve.wait_ge(s["newton"], base + 1)
                    rsqrt(nt[:, 0, 0:4], buf["rq"][:, 2 * (h % 2) + part, :], nt[:, 1, 0:4], s["newton"],
                          base + 1, s["rms"])

                def blocks(k):
                    r, b, hf = k // L.U, L.batches(k)[0], k % 2
                    dve.wait_ge(s["j_out"], L.evac[("k", r, b // 4)])
                    if k >= 2:
                        dve.wait_ge(s["scores"], k - 1)
                    dve.tensor_tensor(
                        buf["kz"][:, k % 2, :].rearrange("p (e t) -> p e t", e=4),
                        buf["kT"][:, r % 2, tokens(b)].unsqueeze(1).to_broadcast([P, 4, P]),
                        buf["bd"][:, hf, :].unsqueeze(2).to_broadcast([P, 4, P]), ALU.mult).then_inc(s["kz"], 1)
                    if k >= 2:
                        dve.wait_ge(s["values"], k - 1)
                    kv = 2 * r + hf
                    dve.wait_ge(s["v_rows"], b // 4 + 1)
                    dve.tensor_copy(buf["vz"][:, k % 2, 112:128], buf["v"][:, b, 16 * kv:16 * kv + 16])\
                        .then_inc(s["vz"], 1)

                normed = False
                for what in L.first:
                    if what[0] == "K":
                        key_rows(what)
                    elif what[0] == "ln":
                        b = what[2]
                        if not normed:
                            norm_stats(norm)
                            if n == 2:
                                dve.wait_ge(s["k_turned"], 2 * B)
                            norm_rows(norm, 0)
                            normed = True
                        if n == 1:
                            rms_rows(s, buf, b, g)
                        elif b + 1 < B:
                            norm_rows(norm, b + 1)
                        norm_lo(norm, b)
                        if n == 1 and b + 1 < B:
                            norm_rows(norm, b + 1)
                    elif what[0] == "q" and n == 2:
                        query_rstd(lambda i: what, 0, None)
                if n == 0:
                    blocks(0)

                def step(k, it):
                    if k < L.NU:
                        h = k // L.U
                        width = L.key_tiles * P
                        rows = D // width
                        bank_ = S[k % 2][:, :].rearrange("p (j t) -> p j t", j=rows)
                        pr = probs[:, k % 2, :].rearrange("p (j t) -> p j t", j=rows)
                        dve.wait_ge(s["scores"], at(L, lambda i: i + 1, k, it))
                        if n in (1, 2) and k >= 2:
                            dve.wait_ge(s["turned"], at(L, lambda i: i - 1, k, it))
                        if n == 1:
                            hh = at(L, lambda i: i // L.U, k, it)
                            pb = buf["pb"][:, hh:hh + 1, :] if it is None else buf["pb"][:, bass.ds(hh, 1), :]
                            dve.tensor_tensor(pr, bank_, pb.to_broadcast([P, 4, P]), ALU.add).then_inc(s["seen"], 1)
                            dve.wait_ge(s["seen"], at(L, lambda i: i + 1, k, it))
                            b0 = L.batches(k)[0]
                            dve.tensor_tensor(pr, pr, buf["m"][:, b0:b0 + 4, :], ALU.add).then_inc(s["masked"], 1)
                            dve.wait_ge(s["masked"], at(L, lambda i: i + 1, k, it))
                            dve.tensor_reduce(top[:, k % 2, :], pr, AX_X, ALU.max, negate=True).then_inc(s["clamp"], 1)
                            dve.wait_ge(s["clamp"], at(L, lambda i: i + 1, k, it))
                            dve.tensor_scalar(top[:, k % 2, :], top[:, k % 2, :], MASKED / 10, None, ALU.min)\
                                .then_inc(s["top"], 1)
                        elif n == 2:
                            dve.wait_ge(s["rms"], at(L, lambda i: L.rstd[("q", i // L.U, i % 2)], k, it))
                            for j in range(4):
                                o = dve.scalar_tensor_tensor(
                                    out=pr[:, j, :], in0=bank_[:, j, :],
                                    scalar=buf["rq"][:, 2 * (h % 2) + k % 2, j:j + 1],
                                    in1=buf["madd"][:, :], op0=ALU.mult, op1=ALU.add)
                            o.then_inc(s["seen"], 1)
                            dve.wait_ge(s["seen"], at(L, lambda i: i + 1, k, it))
                            dve.tensor_reduce(top[:, k % 2, :], pr, AX_X, ALU.max, negate=True).then_inc(s["top"], 1)
                        else:
                            dve.tensor_reduce(top[:, k % 2, 0:rows], bank_, AX_X, ALU.max, negate=True)\
                                .then_inc(s["top"], 1)
                        if n == 0 and k + 1 < L.NU:
                            blocks(k + 1)
                        dve.wait_ge(s["exp"], at(L, lambda i: i + 1, k, it))
                        if n == 1:
                            dve.tensor_scalar(sums[:, k % 2, :], sums[:, k % 2, :], 1e-30, None, ALU.max)\
                                .then_inc(s["sum"], 1)
                            dve.wait_ge(s["sum"], at(L, lambda i: i + 1, k, it))
                        dve.reciprocal(inv[:, k % 2, 0:rows], sums[:, k % 2, 0:rows]).then_inc(s["inv"], 1)
                        dve.wait_ge(s["inv"], at(L, lambda i: i + 1, k, it))
                        dve.tensor_tensor(pr, pr, inv[:, k % 2, 0:rows].unsqueeze(2).to_broadcast([P, rows, width]),
                                          ALU.mult).then_inc(s["probs"], 1)
                    if L.has_O(k):
                        for j, b in enumerate(L.out_batches(k - 2)):
                            no_f = (lambda i, j=j: L.tile[(i - 2, L.out_batches(i - 2)[j])])
                            dve.wait_ge(s["outp"], at(L, no_f, k, it))
                            if no_f(k) > B:
                                dve.wait_ge(s["x_acc"], at(L, lambda i: no_f(i) - B, k, it))
                            dve.scalar_tensor_tensor(out=x[:, b, :], in0=O[no_f(k) % 2][:, :], scalar=g,
                                                     in1=x[:, b, :], op0=ALU.mult, op1=ALU.add)\
                                .then_inc(s["x_acc"], 1)
                    if n == 2:
                        for j in range(len(L.pieces(k))):
                            query_rstd(lambda i: L.pieces(i)[0], k, it)
                    if 1 <= k <= L.NU and not (n == 0 and k % 2 == 1):
                        f = (lambda i: i // 2) if n == 0 else (lambda i: i)
                        dve.wait_ge(s["a_hi"], at(L, f, k, it))
                        w = L.nb * P
                        o = (k // 2 - 1) % 2 * P if n == 0 else 0
                        dve.tensor_tensor(buf["a_lo"][:, 0:w], V[:, o:o + w], f32(buf["a_hi"][:, 0:w]),
                                          ALU.subtract).then_inc(s["a_lo"], 1)

                if n == 1:
                    dve.wait_ge(pb_in, 16)
                    dve.wait_ge(s["m_ready"], 1)
                run_steps(dve, L, step)

            def rms_rows(s, buf, b, g):
                dve.wait_ge(ln_rows, B * LN2 + b + 1)
                dve.scalar_tensor_tensor(out=x[:, b, :], in0=probs[:, b % 2, :], scalar=g, in1=x[:, b, :],
                                         op0=ALU.mult, op1=ALU.add).then_inc(s["added"], 1)
                dve.wait_ge(ln_sq, b + 1)
                base = 12 * b
                dve.tensor_scalar(nt[:, 0, 0:1], buf["r2"][:, b:b + 1], 1.0 / D, EPS, ALU.mult, ALU.add)\
                    .then_inc(s["r2"], 1)
                dve.wait_ge(s["r2"], base + 1)
                rsqrt(nt[:, 0, 0:1], nt[:, 2, 0:1], nt[:, 1, 0:1], s["r2"], base + 1, None)
                dve.scalar_tensor_tensor(out=probs[:, b % 2, :], in0=probs[:, b % 2, :], scalar=nt[:, 2, 0:1],
                                         in1=buf["ln_w"][:, :], op0=ALU.mult, op1=ALU.mult).then_inc(ln_y, 1)

            def norm_all(n):
                norm_stats(n)
                norm_rows(n, 0)
                for b in range(B):
                    if b + 1 < B:
                        norm_rows(n, b + 1)
                    norm_lo(n, b)

            def mixture(n):
                s, buf, norm = FS[n], MIX[n], 2 * n + 1
                g = gate[:, 4 + n:5 + n]
                norm_all(norm)
                tiny = [0]

                def then(ins):
                    tiny[0] += 1
                    ins.then_inc(s["tiny"], 1)
                    dve.wait_ge(s["tiny"], tiny[0])

                def over_experts(v):
                    return v.unsqueeze(2).to_broadcast([P, B, 8])

                pr, pw, s1, s2 = (buf[k][:, :, :] for k in ("pr", "pw", "s1", "s2"))
                red, red2 = buf["red"][:, 0, :], buf["red"][:, 1, :]
                then(dve.memset(buf["sx"][:, :, :], 0.0))
                if n == 0:
                    dve.wait_ge(phase_in["F0"], 16)
                else:
                    for e in range(8):
                        then(dve.memset(buf["ex"][:, e:e + 1], float(8 - e)))
                dve.wait_ge(s["l_turned"], 1)
                logits = T[:, 0:8 * B].rearrange("p (b e) -> p b e", e=8)
                if n == 0:
                    then(dve.tensor_tensor(pr, logits, buf["ex"][:, :].unsqueeze(1).to_broadcast([P, B, 8]),
                                           ALU.add))
                else:
                    then(dve.tensor_copy(pr, logits))
                then(dve.tensor_reduce(red, pr, AX_X, ALU.max))
                dve.tensor_tensor(pr, pr, over_experts(red), ALU.subtract).then_inc(s["probs"], 1)

                def add_out(no, b, before=None):
                    dve.wait_ge(s["outp"], no)
                    if before:
                        dve.wait_ge(s["x_acc"], before)
                    dve.scalar_tensor_tensor(out=x[:, b, :], in0=O[b % 2][:, :], scalar=g, in1=x[:, b, :],
                                             op0=ALU.mult, op1=ALU.add).then_inc(s["x_acc"], 1)

                dve.wait_ge(s["s_exp"], 1)
                then(dve.tensor_reduce(red, pr, AX_X, ALU.add))
                then(dve.reciprocal(red2, red))
                then(dve.tensor_tensor(pr, pr, over_experts(red2), ALU.mult))
                if n == 0:
                    then(dve.tensor_scalar(pw, pr, 8.0 * 2.0, None, ALU.mult))
                    rank = 16
                else:
                    order = buf["ex"][:, :].unsqueeze(1).to_broadcast([P, B, 8])

                    def pick(sel, tmp):
                        then(dve.tensor_reduce(red, pw, AX_X, ALU.max))
                        then(dve.tensor_tensor(tmp, pw, over_experts(red), ALU.is_equal))
                        then(dve.tensor_tensor(tmp, tmp, order, ALU.mult))
                        then(dve.tensor_reduce(red2, tmp, AX_X, ALU.max))
                        then(dve.tensor_tensor(sel, tmp, over_experts(red2), ALU.is_equal))

                    then(dve.tensor_copy(pw, pr))
                    pick(s1, s2)
                    then(dve.scalar_tensor_tensor(out=pw, in0=s1, scalar=-4.0, in1=pr, op0=ALU.mult, op1=ALU.add))
                    pick(s2, s2)
                    then(dve.tensor_tensor(s1, s1, s2, ALU.add))
                    then(dve.tensor_tensor(pw, pr, s1, ALU.mult))
                    then(dve.tensor_reduce(red, pw, AX_X, ALU.add))
                    then(dve.reciprocal(red2, red))
                    then(dve.tensor_tensor(pw, pw, over_experts(red2), ALU.mult))
                    then(dve.tensor_scalar(pw, pw, 2.0, None, ALU.mult))
                    rank = 8
                for b in range(B):
                    o = dve.tensor_copy(buf["sx"][:, b, 0:8 * rank].rearrange("p (e r) -> p e r", e=8),
                                        pw[:, b, :].unsqueeze(2).to_broadcast([P, 8, rank]))
                o.then_inc(s["sx"], 1)
                outs = 0
                if n == 1:
                    for b in range(B):
                        add_out(b + 1, b)
                    outs = B
                dve.wait_ge(s["low"], 4)
                for t in range(2):
                    dve.wait_ge(s["s_turned"], t + 1)
                    dve.tensor_tensor(buf["hm"][:, half(t)], TV[t][:, :], buf["lowT"][:, half(t)], ALU.mult)\
                        .then_inc(s["hm"], 1)
                for t in range(2):
                    dve.wait_ge(s["h_hi"], t + 1)
                    dve.tensor_tensor(buf["h_lo"][:, half(t)], buf["hm"][:, half(t)],
                                      f32(buf["h_hi"][:, half(t)]), ALU.subtract).then_inc(s["h_lo"], 1)
                for b in range(B):
                    add_out(outs + b + 1, b, b + 1 if outs else None)

            def swiglu():
                s, norm = FS[2], 5
                g = gate[:, 6:7]
                norm_all(norm)
                for t in range(2):
                    dve.wait_ge(s["low_hi"], t + 1)
                    dve.tensor_tensor(M2["low_lo"][:, half(t)], J[t][:, :], f32(M2["low_hi"][:, half(t)]),
                                      ALU.subtract).then_inc(s["low_lo"], 1)
                for j in range(HIDDEN_TILES + 1):
                    if j < HIDDEN_TILES:
                        for t in range(2):
                            no = 2 * j + t
                            dve.wait_ge(s["silu"], no + 1)
                            dve.wait_ge(s["proj"], 2 + 2 * no + 2)
                            if no >= 2:
                                dve.wait_ge(s["h_hi"], no - 1)
                            dve.tensor_tensor(M2["hid"][:, t, :], (J if t == 0 else S)[1][:, :],
                                              M2["sg"][:, t, :], ALU.mult).then_inc(s["hid"], 1)
                            dve.wait_ge(s["h_hi"], no + 1)
                            dve.tensor_tensor(M2["h_lo"][:, j % 2, half(t)], M2["hid"][:, t, :],
                                              f32(M2["h_hi"][:, j % 2, half(t)]), ALU.subtract)\
                                .then_inc(s["h_lo"], 1)
                    if j == 0:
                        continue
                    if j == HIDDEN_TILES:
                        for t in range(2):
                            dve.wait_ge(s["dl_hi"], t + 1)
                            dve.tensor_tensor(M2["dl_lo"][:, half(t)], TV[t][:, :],
                                              f32(M2["dl_hi"][:, half(t)]), ALU.subtract).then_inc(s["dl_lo"], 1)
                    for b in range(B):
                        add_tile(s, g, (j - 1) * B + b + 1, b)
                for b in range(B):
                    add_tile(s, g, HIDDEN_TILES * B + b + 1, b)

            def add_tile(s, g, no, b):
                dve.wait_ge(s["outp"], no)
                if no > B:
                    dve.wait_ge(s["x_acc"], no - B)
                dve.scalar_tensor_tensor(out=x[:, b, :], in0=O[b % 2][:, :], scalar=g, in1=x[:, b, :],
                                         op0=ALU.mult, op1=ALU.add).then_inc(s["x_acc"], 1)

            def quantised():
                s, norm = FS[3], 7
                g = gate[:, 7:8]
                dve.wait_ge(*ADDS[norm - 1])
                dve.wait_ge(phase_in["F3"], 64)
                codes = M3["u"][:, :, :].rearrange("p n (g c) -> p n g c", c=4)
                words = M3["qw"][:, :, :].rearrange("p n (g c) -> p n g c", c=3)
                for c, (w, shift) in enumerate(((0, 0), (0, 6), (1, 0), (2, 0))):
                    dve.tensor_scalar(codes[:, :, :, c], words[:, :, :, w], shift, 63,
                                      ALU.logical_shift_right, ALU.bitwise_and).then_inc(s["codes"], 1)
                dve.wait_ge(s["codes"], 4)
                for nt_ in range(KT):
                    dve.tensor_scalar(M3["wn"][:, nt_, :], M3["u"][:, nt_, :], M3["zp"][:, nt_:nt_ + 1],
                                      M3["sc"][:, nt_:nt_ + 1], ALU.subtract, ALU.mult).then_inc(s["wn"], 1)
                for kt in range(KT):
                    dve.wait_ge(s["wT_hi"], kt + 1)
                    dve.tensor_tensor(M3["wT_lo"][:, kt, :], (J + S)[kt][:, :], f32(M3["wT_hi"][:, kt, :]),
                                      ALU.subtract).then_inc(s["wT_lo"], 1)
                norm_all(norm)
                for b in range(B):
                    dve.scalar_tensor_tensor(out=x[:, b, :], in0=M3["bias"][:, :], scalar=g, in1=x[:, b, :],
                                             op0=ALU.mult, op1=ALU.add).then_inc(s["x_acc"], 1)
                    dve.wait_ge(s["outp"], b + 1)
                    dve.wait_ge(s["x_acc"], 2 * b + 1)
                    dve.scalar_tensor_tensor(out=x[:, b, :], in0=O[b % 2][:, :], scalar=g, in1=x[:, b, :],
                                             op0=ALU.mult, op1=ALU.add).then_inc(s["x_acc"], 1)

            attention(0)
            mixture(0)
            attention(1)
            mixture(1)
            attention(2)
            swiglu()
            attention(3)
            quantised()


def by_feature_chunk(w_t, m, width=P):
    out = np.zeros((P, KT, P), w_t.dtype)
    out[:, :, :width] = w_t[:, m * width:(m + 1) * width].reshape(KT, P, width).transpose(1, 0, 2)
    return out.reshape(P, D)


def by_token_chunk(w_t, g, kt):
    return w_t[kt * P:(kt + 1) * P, g * D:(g + 1) * D]


def rows_chunk(w, r):
    out = np.zeros((P, D), w.dtype)
    part = w[r * P:(r + 1) * P]
    out[:len(part)] = part
    return out


def lay_out_stream(a):
    t = {k: np.ascontiguousarray(v.T) for k, v in a.items() if k in (
        "L1_xattn_w_q", "L1_xattn_w_k", "L1_xattn_w_v", "L1_xattn_w_out", "L2_xattn_q_proj_w",
        "L2_xattn_k_proj_w", "L2_xattn_v_proj_w", "L2_xattn_o_proj_w", "L1_ffn_W_base", "L0_ffn_Wr",
        "L1_ffn_gate_W", "L2_ffn_gate_w", "L2_ffn_up_w", "L2_ffn_down_w", "L2_ffn_gate_a",
        "L2_ffn_up_a", "L2_ffn_down_a", "L2_ffn_gate_b", "L2_ffn_up_b", "L2_ffn_down_b")}
    wk_rep = np.repeat(a["L0_xattn_Wk"].reshape(D, 8, 1, 16), 4, axis=2).reshape(D, D)
    low_a = [a[f"L{n}_ffn_A"].reshape(-1, D).T for n in range(2)]
    low_b = [a[f"L{n}_ffn_B"].transpose(0, 2, 1).reshape(-1, D) for n in range(2)]

    def chunk(phase, c):
        kind, i = c[0], c[1:]
        if phase == "L0":
            w = {"q": a["L0_xattn_Wq"], "k": wk_rep, "v0": a["L0_xattn_Wv"]}
            return rows_chunk(a["L0_xattn_Wo"], i[0]) if kind == "o" else by_feature_chunk(w[kind], i[0])
        if phase == "L1":
            if kind == "v":
                return by_token_chunk(t["L1_xattn_w_v"], *i)
            if kind == "o":
                return rows_chunk(t["L1_xattn_w_out"], i[0])
            return by_feature_chunk(t[f"L1_xattn_w_{kind}"], i[0])
        if phase == "L2":
            if kind in ("K", "V"):
                return by_token_chunk(t[f"L2_xattn_{kind.lower()}_proj_w"], *i)
            if kind == "o":
                return rows_chunk(t["L2_xattn_o_proj_w"], i[0])
            return by_feature_chunk(t["L2_xattn_q_proj_w"], i[0])
        if phase == "L3":
            if kind == "V":
                return by_token_chunk(a["L3_xattn_Wv"], *i)
            if kind == "o":
                return rows_chunk(a["L3_xattn_Wo"], i[0])
            return by_feature_chunk(a[f"L3_xattn_W{kind.lower()}"], i[0])
        if phase in ("F0", "F1"):
            n = int(phase[1])
            if kind == "R":
                return by_feature_chunk(t["L0_ffn_Wr" if n == 0 else "L1_ffn_gate_W"], 0, 8)
            if kind == "A":
                return by_feature_chunk(low_a[n], 0, low_a[n].shape[1])
            if kind == "B":
                return rows_chunk(low_b[n], 0)
            return by_token_chunk(t["L1_ffn_W_base"], 0, i[0])
        if kind == "A":
            return by_feature_chunk(np.concatenate([t["L2_ffn_gate_a"], t["L2_ffn_up_a"]], 1), 0, 32)
        if kind == "b":
            return rows_chunk(t["L2_ffn_down_b"], 0)
        j = i[0]
        n = min(P, t["L2_ffn_gate_w"].shape[1] - j * P)
        cols = slice(j * P, j * P + n)
        if kind in ("g", "u"):
            w = t["L2_ffn_gate_w" if kind == "g" else "L2_ffn_up_w"]
            return by_feature_chunk(w[:, cols], 0, n)
        if kind == "d":
            return rows_chunk(t["L2_ffn_down_w"], j)
        out = np.zeros((P, D), w_dtype)
        out[0:16, 0:n] = t["L2_ffn_gate_b"][:, cols]
        out[16:32, P:P + n] = t["L2_ffn_up_b"][:, cols]
        out[0:n, 2 * P:2 * P + 16] = t["L2_ffn_down_a"][cols, :]
        return out

    w_dtype = a["L0_xattn_Wq"].dtype
    stream = np.zeros((STREAM_LEN, P, D), w_dtype)
    for no, (phase, c) in enumerate(STREAM):
        stream[no] = chunk(phase, c)
    return stream


def kernel(**inputs):
    import concourse.bacc as bacc
    from concourse.bass_utils import run_bass_kernel_spmd

    a = {k: np.asarray(v) for k, v in inputs.items()}

    def rows(v):
        return np.ascontiguousarray(np.broadcast_to(v.reshape(1, -1), (P, v.size)))

    arrays = {
        "x_in": a["x"],
        "ctx_t": np.ascontiguousarray(a["ctx_4096"].reshape(TOK, D).T.reshape(KT, P, TOK)),
        "mask": np.ascontiguousarray(a["mask_BxSxS2_bk0"].transpose(1, 0, 2)).view(np.uint32),
        "mask_add": a["mask_1x1xSxS2_ff0"].reshape(P, P),
        "gates": rows(np.concatenate([a["g_xattn"], a["g_ffn"]])),
        "stream": lay_out_stream(a),
        "lora_bias": rows(a["L0_ffn_br"]),
        "position_bias": np.ascontiguousarray(a["L1_xattn_position_bias"].transpose(1, 0, 2)),
        "ln_weight": rows(a["L1_xattn_ln_weight"]),
        "qk_norm": np.ascontiguousarray(np.stack([a["L2_xattn_q_norm_w"], a["L2_xattn_k_norm_w"]], 1)),
        "qweight": np.ascontiguousarray(a["L3_ffn_qweight"].reshape(KT, P, 384).transpose(1, 0, 2)),
        "q_scale": np.ascontiguousarray(a["L3_ffn_weight_scale"].reshape(KT, P).T),
        "q_zero": np.ascontiguousarray(a["L3_ffn_weight_zero_point"].reshape(KT, P).T),
        "q_bias": rows(a["L3_ffn_bias"]),
    }
    nc = bacc.Bacc("TRN2", target_bir_lowering=False, num_devices=1)
    arrays = {f"in_{k}": np.ascontiguousarray(v) for k, v in arrays.items()}
    args = [nc.dram_tensor(k, v.shape, mybir.dt.from_np(v.dtype), kind="ExternalInput").ap()
            for k, v in arrays.items()]
    out = nc.dram_tensor("out_0", (B, P, D), F32, kind="ExternalOutput").ap()
    build(nc, *args, out)
    r = run_bass_kernel_spmd(nc, [arrays], core_ids=[0])
    return r.results[0]["out_0"]
```

```python
from contextlib import ExitStack

import numpy as np

import concourse.bass as bass
from concourse import mybir

F32 = mybir.dt.float32
F32R = mybir.dt.float32r
I32 = mybir.dt.int32
U8 = mybir.dt.uint8
U32 = mybir.dt.uint32
ALU = mybir.AluOpType
ACT = mybir.ActivationFunctionType
AX_X = mybir.AxisListType.X

P = 128
B = 8
D = 512
KT = D // P
TOK = B * P
HALF = TOK // 2
HEADS = 32
EPS = 1e-5
RAW = 2
RING = 8
HIDDEN_TILES = 11
MASKED = 1e30


EARLY = {"L0": 0, "L1": 4, "L2": 8, "L3": 8}


class Attention:

    def __init__(self, name, heads, units, period):
        self.name = name
        self.heads = heads
        self.U = units
        self.NU = heads * units
        self.period = period
        self.nb = 1 if name == "L0" else B // units
        self.key_tiles = 2 if name == "L3" else 1
        self.group = 4
        self.lag_v = 2 if name == "L0" else 1
        self.lag_o = self.lag_v + 1
        self.steps = self.NU + self.lag_o
        self.piece = {}
        self.tile = {}
        self.rstd = {}
        self.evac = {}
        self.order = []
        self.prologue()
        for i in range(self.steps):
            if name != "L2":
                for what in self.pieces(i):
                    self.count_piece(what)
            if self.has_O(i):
                u = i - self.lag_o
                for b in self.batches(u):
                    self.tile[(u, b)] = len(self.tile) + 1
                if u % self.U == self.U - 1:
                    self.order.append(("o", u // self.U))
            if name == "L2":
                for what in self.pieces(i):
                    self.count_piece(what)
            for what in self.value_pieces(i):
                self.count_piece(what)
        self.chunk = {c: n for n, c in enumerate(self.order)}

    def count_piece(self, what):
        kind, h, part = what
        self.piece[what] = len(self.piece) + 1
        if kind != "K":
            self.evac[what] = len(self.evac) + 1
        if kind in ("q", "K") and self.name == "L2":
            self.rstd[what] = len(self.rstd) + 1
        if kind in ("q", "k") and part == 1:
            self.order.append((kind, h))
        if kind == "v" and part == B - 1:
            self.order += [("v", h, kt) for kt in range(KT)]

    def prologue(self):
        both, tiles = range(2), range(B)
        norm = [("ln", 0, b) for b in tiles]
        q = [("q", 0, t) for t in both]
        if self.name == "L0":
            self.first = [("v0", 0, t) for t in both] + [("k", 0, t) for t in both] + norm[:5]
            self.first += [q[0]] + norm[5:] + [q[1]]
        if self.name == "L1":
            v = [("v", 0, b) for b in tiles]
            self.first = [("k", 0, t) for t in both] + v[:6] + [norm[0], v[6]] + norm[1:5]
            self.first += [q[0], norm[5], v[7], norm[6], norm[7], q[1]]
        if self.name == "L2":
            v = [("V", 1, b) for b in tiles]
            self.first = [(kind, g, b) for kind, g in (("V", 0), ("K", 0), ("K", 1)) for b in tiles]
            self.first += v[:2] + [w for j in range(5) for w in (v[2 + j], norm[j])]
            self.first += [q[0], norm[5], v[7], norm[6], norm[7], q[1]]
        if self.name == "L3":
            self.first = [("Vc", 0, b) for b in tiles]
            kc = [("Kc", g, t) for g in range(4) for t in both]
            self.first += kc[:3] + [w for b in range(5) for w in (norm[b], kc[3 + b])] + norm[5:]
            self.first += [("Kx", g, t) for g in range(4) for t in both]
            vx, w = [("Vx", 0, b) for b in tiles], [("w", 0, kt) for kt in range(KT)]
            self.first += vx[:4] + [w[0], w[1]] + vx[4:6] + [w[2], w[3]] + vx[6:] + q
        self.early = EARLY[self.name]
        for what in self.first:
            kind, h, part = what
            if kind in ("ln", "w"):
                continue
            self.count_piece(what)
            if kind == "v0" and part == 1:
                self.order.append(("v0", 0))
            if kind in ("K", "V", "Vc") and part == B - 1:
                self.order += [(kind, h, kt) for kt in range(KT)]
            if kind == "Kx" and part == 1:
                self.order.append(("K", h))
            if kind == "Vx" and part == B - 1:
                self.order += [("V", 0, kt) for kt in range(KT)]

    def early_chunks(self):
        return self.order[:{"L0": 0, "L1": 1, "L2": KT, "L3": KT}[self.name]]

    def parts(self, i):
        t = i % self.U
        if i >= self.NU or i // self.U + 1 >= self.heads:
            return []
        if self.name == "L0":
            return [("k" if t < 8 else "q", t % 8 // 4, t % 4, 1)]
        if self.name == "L1":
            return [("q", t, 0, KT), ("k", t, 0, KT)]
        if self.name == "L2":
            return [("q", t, 0, KT - 1), ("q", t, KT - 1, 1)]
        return [("q", t // 2, t % 2 * 2, 2)]

    def pieces(self, i):
        return [(kind, i // self.U + 1, half) for kind, half, kt, n in self.parts(i) if kt + n == KT]

    def value_pieces(self, i):
        if self.name != "L1":
            return []
        period = self.group * self.U
        if i % period == period - 1 and i < self.NU - 1:
            return [("v", i // period + 1, b) for b in range(B // 2)]
        if i % period == 0 and 0 < i < self.NU:
            return [("v", i // period, b) for b in range(B // 2, B)]
        return []

    def batches(self, i):
        if self.name == "L0":
            return [i % self.U // 2]
        t = i % self.U
        return list(range(t * self.nb, (t + 1) * self.nb))

    def has_O(self, i):
        u = i - self.lag_o
        return 0 <= u < self.NU and (self.name != "L0" or u % 2 == 1)

    def has_V(self, i):
        return 0 <= i - self.lag_v < self.NU

    def lead(self):
        if not self.period:
            return self.steps, 0
        lead = 10 if self.name == "L1" else 2
        return lead, (self.NU - lead) // self.period


def at(layer, f, k, it):
    if it is None:
        return f(k)
    grows = f(k + layer.period) - f(k)
    assert all(f(k + n * layer.period) == f(k) + n * grows for n in range(layer.lead()[1]))
    return f(k) + it * grows


def run_steps(engine, layer, step):
    lead, iterations = layer.lead()
    for k in range(lead):
        step(k, None)
    if iterations:
        with engine.Fori(0, iterations) as it:
            for k in range(lead, lead + layer.period):
                step(k, it)
    for k in range(lead + iterations * layer.period, layer.steps):
        step(k, None)


ATT = [Attention("L0", 4, 16, 0), Attention("L1", HEADS, 2, 8),
       Attention("L2", HEADS, 2, 8), Attention("L3", HEADS, 4, 32)]
MLP_ORDER = {
    0: [("R",), ("A",), ("B",)],
    1: [("A",)] + [("W", kt) for kt in range(KT)] + [("B",)],
    2: [("A",), ("g", 0), ("u", 0)] + [c for j in range(HIDDEN_TILES) for c in
                                       [("l", j)]
                                       + ([("g", j + 1), ("u", j + 1)] if j + 1 < HIDDEN_TILES else [])
                                       + [("d", j)]] + [("b",)],
    3: [],
}


NORM_ORDER = {
    n: [("early", 2), ("early", 3), ("ln", 0)]
    + [w for j in range(1, 5) for w in ((("early", 3 + j),) if n and j < 4 else ()) + (("ln", j),)]
    + [("A" if n else "R", 0), ("ln", 5)] + ([("early", 7)] if n else []) + [("ln", 6), ("ln", 7), ("A" if n else "R", 1)]
    for n in range(3)}


def stream_order():
    out = []
    for n in range(4):
        L = ATT[n]
        order = [(L.name, c) for c in L.order if c not in L.early_chunks()]
        if n < 3:
            early = [(ATT[n + 1].name, c) for c in ATT[n + 1].early_chunks()]
            if n == 0:
                order[-1:-1] = early
            else:
                order += early
        out += order
        out += [(f"F{n}", c) for c in MLP_ORDER[n]]
    return out


STREAM = stream_order()
CHUNK_AT = {c: n for n, c in enumerate(STREAM)}
STREAM_LEN = -(-len(STREAM) // RING) * RING


def build(nc, x_in, ctx_t, mask, mask_add, gates, stream, lora_bias, position_bias, ln_weight,
          qk_norm, qweight, q_scale, q_zero, q_bias, out):
    ctx = ExitStack()
    with ctx:
        def sb(name, shape, dt=F32, stack=ctx):
            return stack.enter_context(nc.sbuf_tensor(name, shape, dt))

        def sem(name):
            return ctx.enter_context(nc.semaphore(name))

        M3 = {}
        with ExitStack() as st:
            ct_hi = sb("ct_hi", [P, KT, TOK], F32R, st)
            ct_lo = sb("ct_lo", [P, KT, TOK], F32R, st)
        M3["wT_hi"] = sb("wT_hi", [P, KT, D], F32R)
        M3["wT_lo"] = sb("wT_lo", [P, KT, D], F32R)
        with ExitStack() as st:
            M3["u"] = sb("u", [P, KT, D], I32, st)
        M3["bias"] = sb("q_bi", [P, D])
        sb("behind_bias", [P, (KT - 1) * D])
        with ExitStack() as st:
            M3["qw"] = sb("qw", [P, KT, 384], I32, st)
        M3["wn"] = sb("wn", [P, KT, D])

        x = sb("x", [P, B, D])
        xt_hi = sb("xt_hi", [P, KT, TOK], F32R)
        xt_lo = sb("xt_lo", [P, KT, TOK], F32R)
        w_hi = sb("w_hi", [P, RING, D], F32R)
        w_lo = sb("w_lo", [P, RING, D], F32R)
        raw = sb("raw", [P, RAW, D])
        probs = sb("probs", [P, 2, D])
        ident = sb("ident", [P, P])
        ones = sb("ones", [P, 2])
        zero = sb("zero", [P, 1])
        gate = sb("gate", [P, 8])
        stats = sb("stats", [P, B, 6])
        mv = sb("mv", [P, B, 2])
        rstd = sb("rstd", [P, B])
        nt = sb("nt", [P, 3, B])
        top = sb("top", [P, 2, 4])
        sums = sb("sums", [P, 2, 4])
        inv = sb("inv", [P, 2, 4])

        def attention_buffers(stack, n):
            return {
                "qT": sb(f"qT{n}", [P, 2, TOK], F32, stack),
                "pT": sb(f"pT{n}", [P, 1 if n else 2, D], F32, stack),
                "a_hi": sb(f"a_hi{n}", [P, D], F32R, stack),
                "a_lo": sb(f"a_lo{n}", [P, D], F32R, stack),
            }

        with ExitStack() as st:
            A0 = attention_buffers(st, 0)
            A0["kT"] = sb("kT0", [P, 2, TOK], F32, st)
            A0["vT"] = sb("vT0", [P, TOK], F32, st)
            A0["v"] = sb("v0", [P, B, P], F32, st)
            A0["kz"] = sb("kz", [P, 2, D], F32, st)
            A0["vz"] = sb("vz", [P, 2, 240], F32, st)
            A0["bd"] = sb("bd", [P, 2, 4], F32, st)
            A0["ctx_raw"] = sb("ctx_raw", [P, KT, TOK], F32, st)
        with ExitStack() as st:
            A1 = attention_buffers(st, 1)
            A1["ln_w"] = sb("ln_w", [P, D], F32, st)
            A1["m8"] = sb("m8", [P, B, P // 4], U32, st)
            A1["m"] = sb("m", [P, B, P], F32, st)
            sb("behind_F0", [P, 2 * D + D // 4], F32, st)
            A1["kT"] = sb("kT1", [P, 2, TOK], F32, st)
            A1["v"] = sb("v1", [P, B, D], F32, st)
            A1["pb"] = sb("pb", [P, HEADS, P], F32, st)
        with ExitStack() as st:
            A2 = attention_buffers(st, 2)
            A2["kT"] = sb("kT2", [P, 8, TOK], F32, st)
            A2["v"] = sb("v2", [P, B, 2 * D], F32, st)
            A2["vc"] = sb("vc2", [P, B, P], F32, st)
            A2["sq"] = sb("sq2", [P, D], F32, st)
            A2["madd"] = sb("madd", [P, P], F32, st)
            A2["rq"] = sb("rq", [P, 4, 4], F32, st)
            A2["rk"] = sb("rk", [P, 2, 8], F32, st)
            A2["qk_w"] = sb("qk_w", [P, 2], F32, st)
        with ExitStack() as st:
            A3 = attention_buffers(st, 3)
            A3["kT"] = sb("kT3", [P, 4, B, 2 * P], F32, st)
            A3["v"] = sb("v3", [P, 2, B, D], F32, st)
            A3["vc"] = sb("vc3", [P, 2, B, P], F32, st)
            M3["sc"] = sb("q_sc", [P, KT], F32, st)
            M3["zp"] = sb("q_zp", [P, KT], F32, st)
        BUF = [A0, A1, A2, A3]

        def mixture_buffers(n):
            with ExitStack() as st:
                return {
                    "lgT": sb(f"lgT{n}", [P, TOK], F32, st), "lowT": sb(f"lowT{n}", [P, TOK], F32, st),
                    "pr": sb(f"pr{n}", [P, B, 8], F32, st), "pw": sb(f"pw{n}", [P, B, 8], F32, st),
                    "s1": sb(f"s1{n}", [P, B, 8], F32, st), "s2": sb(f"s2{n}", [P, B, 8], F32, st),
                    "ex": sb(f"ex{n}", [P, 8], F32, st), "red": sb(f"red{n}", [P, 2, B], F32, st),
                    "sx": sb(f"sx{n}", [P, B, P], F32, st), "hm": sb(f"hm{n}", [P, TOK], F32, st),
                    "h_hi": sb(f"h_hi{n}", [P, TOK], F32R, st), "h_lo": sb(f"h_lo{n}", [P, TOK], F32R, st),
                }

        LOGITS = {0: slice(0, 8), 1: slice(64, 72)}
        MIX = {0: mixture_buffers(0), 1: mixture_buffers(1)}
        with ExitStack() as st:
            M2 = {
                "low": sb("low", [P, TOK], F32R, st),
                "sg": sb("sg", [P, 2, HALF], F32, st), "hid": sb("hid", [P, 2, HALF], F32, st),
                "h_hi": sb("hid_hi", [P, 2, TOK], F32R, st), "h_lo": sb("hid_lo", [P, 2, TOK], F32R, st),
                "dl": sb("dl", [P, TOK], F32R, st),
            }
        def bank(name):
            return ctx.enter_context(nc.psum_tensor(name, [P, D], F32))

        J = [bank("proj0"), bank("proj1")]
        S = [bank("score0"), bank("score1")]
        T = bank("turned")
        V = bank("value")
        O = [bank("outp0"), bank("outp1")]
        TV = [T, V]
        KEY_BANKS = [S[1], J[1], J[0], S[0]]

        def piece_bank(layer, what):
            no = layer.piece[what]
            return KEY_BANKS[no % 4][:, :] if what[0] == "K" else J[no % 2][:, :]

        raw_in = [sem(f"raw_in{k}") for k in range(RAW)]
        w_hi_done = sem("w_hi_done")
        w_done = sem("w_done")
        w_free = sem("w_free")
        x_in_s = [sem("x_in0"), sem("x_in1")]
        gate_in, pb_in = sem("gate_in"), sem("pb_in")
        ctx_in = [sem(f"ctx_in{kt}") for kt in range(KT)]
        phase_in = {n: sem(f"phase_in{n}") for n in ("F0", "L1", "L2", "F3")}
        setup_done = sem("setup_done")
        gate_done = sem("gate_done")
        ctx_hi_done, ctx_done = sem("ctx_hi_done"), sem("ctx_done")
        stored = sem("stored")
        ln_rows = sem("ln_rows")
        ln_turned = sem("ln_turned")
        ln_hi, ln_lo = sem("ln_hi"), sem("ln_lo")
        ln_tiny = sem("ln_tiny")
        ln_y = sem("ln_y")

        def sems(suffix, names):
            return {name: sem(name + suffix) for name in names.split()}

        common = "scores turned values proj outp j_out exp pT a_hi top inv probs a_lo x_acc"
        AS = [
            sems("_L0", common + " kz vz vt v_rows"),
            sems("_L1", common + " seen masked clamp sum m_ready r2 added"),
            sems("_L2", common + " seen vc qss sq ksum newton rms k_turned k_out wqk"),
            sems("_L3", common + " vc"),
        ]
        FS = [
            sems("_F0", "proj low l_turned probs s_exp sx s_turned hm h_hi h_lo outp x_acc tiny"),
            sems("_F1", "proj low l_turned probs s_exp sx s_turned hm h_hi h_lo outp x_acc tiny"),
            sems("_F2", "proj low_hi low_lo silu hid h_hi h_lo dl dl_hi dl_lo outp x_acc"),
            sems("_F3", "codes wn w_turned wT_hi wT_lo outp biased x_acc"),
        ]

        block = ctx.enter_context(nc.Block())
        SETUP = 8
        KEY_LAG = 3
        DENSE_AHEAD = 6
        RSQRT = 11
        LN2 = 2

        ADDS = []
        for n in range(4):
            ADDS.append((AS[n]["x_acc"], len(ATT[n].tile)))
            ADDS.append((FS[n]["x_acc"], {0: B, 1: 2 * B, 2: (HIDDEN_TILES + 1) * B, 3: B}[n]))

        def phase_start(eng, n):
            if n:
                eng.wait_ge(*ADDS[n - 1])

        def f32(ap):
            return ap.bitcast(F32)

        def tokens(b):
            return slice(b * P, (b + 1) * P)

        def half(t):
            return slice(t * HALF, (t + 1) * HALF)

        def newton_base(layer, what):
            return (RSQRT + 1) * B + RSQRT * (layer.rstd[what] - 1 - 2 * B)

        def chunk_no(layer, what):
            return CHUNK_AT[(layer.name, what)]

        @block.sync
        def _(sp):
            for k in range(RAW):
                sp.dma_start(raw[:, k, :], stream[k]).then_inc(raw_in[k], 16)
            with sp.Fori(0, STREAM_LEN // RAW - 1) as it:
                for k in range(RAW):
                    sp.wait_ge(w_done, it * RAW + (k + 1))
                    sp.dma_start(raw[:, k, :], stream[it * RAW + (RAW + k)]).then_inc(raw_in[k], 16)
            for b in range(B):
                sp.wait_ge(FS[3]["x_acc"], b + 1)
                sp.dma_start(out[b], x[:, b, :]).then_inc(stored, 16)
            sp.wait_ge(stored, 16 * B)

        @block.gpsimd
        def _(pool):
            bd = A0["bd"]
            pool.memset(ident[:, :], 0.0).then_inc(setup_done, 1)
            pool.memset(A0["vz"][:, :, :], 0.0).then_inc(setup_done, 1)
            pool.memset(bd[:, :, :], 1.0).then_inc(setup_done, 1)
            pool.memset(ones[:, :], 1.0).then_inc(setup_done, 1)
            pool.memset(zero[:, :], 0.0).then_inc(setup_done, 1)
            pool.wait_ge(setup_done, 5)
            pool.affine_select(out=ident[:, :], in_=ident[:, :], compare_op=ALU.not_equal, fill=1.0,
                               base=0, pattern=[[-1, P]], channel_multiplier=1).then_inc(setup_done, 1)
            pool.affine_select(out=bd[:, :, :], in_=bd[:, :, :], compare_op=ALU.is_ge, fill=0.0,
                               base=0, pattern=[[-64, 2], [-16, 4]], channel_multiplier=1)\
                .then_inc(setup_done, 1)
            pool.wait_ge(setup_done, 7)
            pool.affine_select(out=bd[:, :, :], in_=bd[:, :, :], compare_op=ALU.is_ge, fill=0.0,
                               base=15, pattern=[[64, 2], [16, 4]], channel_multiplier=-1)\
                .then_inc(setup_done, 1)

            def split(k, chunk_raw, chunk_hi):
                pool.wait_ge(raw_in[k % RAW], chunk_raw)
                pool.tensor_tensor(w_hi[:, k, :], raw[:, k % RAW, :], zero[:, :].to_broadcast([P, D]),
                                   ALU.add)\
                    .then_inc(w_hi_done, 1)
                pool.wait_ge(w_hi_done, chunk_hi)
                pool.tensor_tensor(w_lo[:, k, :], raw[:, k % RAW, :], f32(w_hi[:, k, :]), ALU.subtract)\
                    .then_inc(w_done, 1)

            def split_next(k, it, first):
                pool.wait_ge(w_free, it * RING + (first + k - RING + 1))
                split(k, it * (16 * RING // RAW) + 16 * ((first + k) // RAW + 1), it * RING + (first + k + 1))

            def block_keys(u):
                L, s = ATT[0], AS[0]
                r, b = u // L.U, L.batches(u)[0]
                pool.wait_ge(s["j_out"], L.evac[("k", r, b // 4)])
                if u >= 2:
                    pool.wait_ge(s["scores"], u - 1)
                pool.tensor_tensor(
                    A0["kz"][:, u % 2, :].rearrange("p (e t) -> p e t", e=4),
                    A0["kT"][:, r % 2, tokens(b)].unsqueeze(1).to_broadcast([P, 4, P]),
                    bd[:, u % 2, :].unsqueeze(2).to_broadcast([P, 4, P]), ALU.mult).then_inc(s["kz"], 1)

            for k in range(RING):
                split(k, 16 * (k // RAW + 1), k + 1)
            handed = {}
            for i in range(ATT[0].steps):
                for c in ATT[0].order:
                    if c[0] in "kq" and c[1] and i == c[1] * 16 - (9 if c[0] == "k" else 1):
                        handed[ATT[0].chunk[c]] = i
                    if c[0] == "o" and i == c[1] * 16 + 15 + ATT[0].lag_o:
                        handed[ATT[0].chunk[c]] = i
            late = {}
            for k in range(RING):
                late.setdefault(min(handed.get(k, 0) + 3, ATT[0].NU - 1), []).append(k)
            for u in range(ATT[0].NU):
                block_keys(u)
                for k in late.get(u, []):
                    split_next(k, 0, RING)
            with pool.Fori(0, STREAM_LEN // RING - 2) as it:
                for k in range(RING):
                    split_next(k, it, 2 * RING)

        @block.tensor
        def _(pe):
            owed = [0]

            def mm(out_, l, r, start, stop):
                m = pe.matmul(out_, l, r, start=start, stop=stop, skip_group_check=True)
                return m

            def told(m):
                if owed[0]:
                    m.then_inc(w_free, 1)
                    owed[0] -= 1
                return m

            def mm3(out_, l, r, start, stop, last=False):
                for n, (a, b) in enumerate(((1, 0), (0, 1), (0, 0))):
                    m = mm(out_, l[a], r[b], start and n == 0, stop and n == 2)
                    if not (last and n == 2):
                        told(m)
                return m

            def ring(c, cols=slice(0, D)):
                s = c % RING
                return w_hi[:, s, cols], w_lo[:, s, cols]

            def acts(which, kt, cols):
                hi, lo = (xt_hi, xt_lo) if which == "x" else (ct_hi, ct_lo)
                return hi[:, kt, cols], lo[:, kt, cols]

            def by_feature(dst, c, which, t, kts=range(KT), last=False):
                for kt in kts:
                    m = mm3(dst, ring(c, tokens(kt)), acts(which, kt, half(t)),
                            kt == 0, kt == KT - 1, last and kt == kts[-1])
                return m

            def by_token(dst, cs, which, b, last=False):
                for kt in range(KT):
                    m = mm3(dst, acts(which, kt, tokens(b)), ring(cs[kt]),
                            kt == 0, kt == KT - 1, last and kt == KT - 1)
                return m

            def norm_tile(n, b):
                pe.wait_ge(ln_y if n == 2 else ln_rows, b + 1 if n == 2 else B * n + b + 1)
                if b >= 2:
                    pe.wait_ge(ln_hi, B * n + b - 1)
                    pe.wait_ge(ln_lo, B * n + b - 1)
                for kt in range(KT):
                    m = pe.transpose(TV[b % 2][:, tokens(kt)], probs[:, b % 2, tokens(kt)], ident[:, :])
                m.then_inc(ln_turned, 1)

            def wait_norm(n, tiles):
                pe.wait_ge(ln_hi, B * n + tiles)
                pe.wait_ge(ln_lo, B * n + tiles)

            def early(n, no):
                L, s = ATT[n], AS[n]
                kind, h, part = what = L.first[no]
                if no < 2:
                    pe.wait_ge(AS[n - 1]["j_out"], len(ATT[n - 1].evac))
                    if n == 3:
                        pe.wait_ge(AS[2]["rms"], len(ATT[2].rstd))
                else:
                    pe.wait_ge(s["j_out"], no - 1)
                dst = piece_bank(L, what)
                if kind == "k":
                    pe.wait_ge(w_done, chunk_no(L, (kind, h)) + 1)
                    m = by_feature(dst, chunk_no(L, (kind, h)), "c", part, last=True)
                    owed[0] += part
                else:
                    cs = [chunk_no(L, (kind, h, kt)) for kt in range(KT)]
                    pe.wait_ge(w_done, cs[-1] + 1)
                    m = by_token(dst, cs, "c", part, last=True)
                    if part == B - 1:
                        owed[0] += KT
                m.then_inc(s["proj"], 1)

            def attention(n):
                L, s, buf = ATT[n], AS[n], BUF[n]
                name = L.name
                phase_start(pe, 2 * n)
                if n == 0:
                    pe.wait_ge(setup_done, SETUP)
                by_no = {v: k for k, v in L.piece.items()}

                def bank_free(what_f, k, it):
                    no = L.piece[what_f(k)]
                    if n == 2 and no > 1 and by_no[no - 1][0] == "q":
                        pe.wait_ge(s["newton"], at(L, lambda i: newton_base(
                            L, by_no[L.piece[what_f(i)] - 1]) + 1, k, it))
                    if n == 2 and no <= B + 2 * B + 2:
                        if no > B + 4:
                            pe.wait_ge(s["rms"], no - B - 4)
                    elif no > 2:
                        pe.wait_ge(s["j_out"], at(L, lambda i: L.evac[by_no[L.piece[what_f(i)] - 2]], k, it))

                def chunk(what_f, k, it):
                    pe.wait_ge(w_done, at(L, lambda i: chunk_no(L, what_f(i)) + 1, k, it))
                    return chunk_no(L, what_f(k))

                def chunks(what_f, k, it):
                    chunk(lambda i: (*what_f(i), KT - 1), k, it)
                    return [chunk_no(L, (*what_f(k), kt)) for kt in range(KT)]

                def dst(what):
                    return piece_bank(L, what)

                def first_piece(what):
                    kind, h, part = what
                    bank_free(lambda i: what, 0, None)
                    which = "x" if kind in ("q", "Kx", "Vx") else "c"
                    if which == "x":
                        wait_norm(2 * n, part + 1 if kind == "Vx" else (part + 1) * (B // 2))
                    if kind in ("K", "V", "v", "Vx"):
                        c = chunks(lambda i: (kind[0], h), 0, None)
                        by_token(dst(what), c, which, part, last=True).then_inc(s["proj"], 1)
                        if part == B - 1:
                            owed[0] += KT
                    else:
                        c = chunk(lambda i: ((kind if kind == "v0" else kind[0]), h), 0, None)
                        if kind == "v0" and part == 0:
                            for kt in range(KT):
                                pe.wait_ge(ctx_hi_done, kt + 1)
                                pe.wait_ge(ctx_done, kt + 1)
                                m = by_feature(dst(what), c, which, part, [kt], last=kt == KT - 1)
                        else:
                            m = by_feature(dst(what), c, which, part, last=True)
                        m.then_inc(s["proj"], 1)
                        if part == 1 and kind != "Kc":
                            owed[0] += 1

                def q_squares(what_f, k, it):
                    pe.wait_ge(s["sq"], at(L, lambda i: L.rstd[what_f(i)], k, it))
                    bank_ = J[(L.piece[what_f(k)] + 1) % 2][:, :]
                    for j in range(4):
                        m = mm(bank_[:, 2 * j:2 * j + 2], buf["sq"][:, tokens(j)], ones[:, :], True, True)
                    m.then_inc(s["qss"], 1)

                def turn_keys(what):
                    _, g, b = what
                    no = g * B + b
                    pe.wait_ge(s["rms"], no + 1)
                    if no >= 2:
                        pe.wait_ge(s["k_out"], no - 1)
                    for j in range(4):
                        m = pe.transpose(TV[b % 2][:, tokens(j)], probs[:, b % 2, tokens(j)], ident[:, :])
                    m.then_inc(s["k_turned"], 1)

                for what in L.first[L.early:]:
                    if what[0] == "ln":
                        if n == 0 and what[2] == 0:
                            pe.wait_ge(s["v_rows"], 2)
                        if n == 2 and what[2] == 0:
                            pe.wait_ge(s["k_out"], 2 * B)
                        norm_tile(2 * n, what[2])
                        continue
                    if what[0] == "w":
                        kt = what[2]
                        pe.wait_ge(FS[3]["wn"], 4)
                        if kt >= 2:
                            pe.wait_ge(FS[3]["wT_lo"], kt - 1)
                        for nt in range(KT):
                            m = pe.transpose(S[kt % 2][:, tokens(nt)], M3["wn"][:, nt, tokens(kt)], ident[:, :])
                        m.then_inc(FS[3]["w_turned"], 1)
                        continue
                    first_piece(what)
                    if n == 2 and B + KEY_LAG < L.piece[what] <= B + KEY_LAG + 2 * B:
                        turn_keys(by_no[L.piece[what] - KEY_LAG])
                    if n == 2 and what[0] == "q":
                        q_squares(lambda i: what, 0, None)
                    if what == ("v0", 0, 1):
                        pe.wait_ge(s["j_out"], 2)
                        for b in range(B):
                            m = pe.transpose(TV[b // 4][:, tokens(b % 4)], buf["vT"][:, tokens(b)], ident[:, :])
                        m.then_inc(s["vt"], 1)

                def scores(k, it):
                    h, t = k // L.U, k % L.U
                    kinds = "qk" if n == 1 else "q"
                    pe.wait_ge(s["j_out"], at(L, lambda i: max(
                        L.evac[(kind, i // L.U, L.batches(i)[0] // (B // 2))] for kind in kinds), k, it))
                    if k >= 2:
                        pe.wait_ge(s["seen"] if n in (1, 2) else s["exp"], at(L, lambda i: i - 1, k, it))
                    elif n == 3:
                        pe.wait_ge(FS[3]["wT_lo"], KT)
                    bank_ = S[k % 2]
                    qT = buf["qT"][:, h % 2, :]
                    if n == 0:
                        pe.wait_ge(s["kz"], k + 1)
                        b = L.batches(k)[0]
                        mm(bank_[:, :], qT[:, tokens(b)], buf["kz"][:, k % 2, :], True, True)\
                            .then_inc(s["scores"], 1)
                        return
                    for j, b in enumerate(L.batches(k)):
                        if n == 1:
                            keys = buf["kT"][:, h % 2, tokens(b)]
                        elif n == 2:
                            kv = at(L, lambda i: i // L.U // 4, k, it)
                            keys = buf["kT"][:, kv, tokens(b)] if it is None else \
                                buf["kT"][:, bass.ds(kv, 1), tokens(b)].rearrange("p a k -> p (a k)")
                        else:
                            kv = at(L, lambda i: i // L.U // 8, k, it)
                            keys = buf["kT"][:, kv, b, :] if it is None else \
                                buf["kT"][:, bass.ds(kv, 1), b, :].rearrange("p a k -> p (a k)")
                        w = D // len(L.batches(k))
                        m = mm(bank_[:, j * w:(j + 1) * w], qT[:, tokens(b)], keys, True, True)
                        if b != L.batches(k)[-1]:
                            told(m)
                    m.then_inc(s["scores"], 1)

                def turn(k, it):
                    pe.wait_ge(s["probs"], at(L, lambda i: i + 1, k, it))
                    if k >= 1:
                        pe.wait_ge(s["pT"], at(L, lambda i: i, k, it))
                    for j in range(4):
                        m = pe.transpose(T[:, tokens(j)], probs[:, k % 2, tokens(j)], ident[:, :])
                        if j < 3:
                            told(m)
                    m.then_inc(s["turned"], 1)

                def values(k, it):
                    pe.wait_ge(s["pT"], at(L, lambda i: i + 1, k, it))
                    if n == 0:
                        b, hf = L.batches(k)[0], k % 2
                        pe.wait_ge(s["vz"], k + 1)
                        pair = k // 2
                        if hf == 0 and pair >= 2:
                            pe.wait_ge(s["a_lo"], pair - 1)
                        for e in range(4):
                            lo = 112 - 16 * (4 * hf + e)
                            m = mm(V[:, tokens(pair % 2)], buf["vz"][:, k % 2, lo:lo + P],
                                   buf["pT"][:, k % 2, tokens(e)], hf == 0 and e == 0, hf == 1 and e == 3)
                            if e < 3:
                                told(m)
                        m.then_inc(s["values"], 1)
                        return
                    if k >= 1:
                        pe.wait_ge(s["a_hi"], at(L, lambda i: i, k, it))
                        pe.wait_ge(s["a_lo"], at(L, lambda i: i, k, it))
                    h = k // L.U
                    if n == 1:
                        pe.wait_ge(s["j_out"], at(L, lambda i: L.evac[("v", i // L.U // 4, max(L.batches(i)))],
                                               k, it))
                    else:
                        per = 4 if n == 2 else 8
                        pe.wait_ge(s["vc"], at(L, lambda i: i // L.U // per + 1, k, it))
                    for j, b in enumerate(L.batches(k)):
                        for kt in range(L.key_tiles):
                            if n == 1:
                                v = buf["v"][:, b, tokens(h % 4)]
                            elif n == 2:
                                v = buf["vc"][:, b, :]
                            else:
                                v = buf["vc"][:, kt, b, :]
                            m = mm(V[:, tokens(j)], v, buf["pT"][:, 0, tokens(j * L.key_tiles + kt)],
                                   kt == 0, kt == L.key_tiles - 1)
                            if not (b == L.batches(k)[-1] and kt == L.key_tiles - 1):
                                told(m)
                    m.then_inc(s["values"], 1)

                def output(k, it, tiles=range(B)):
                    c = chunk(lambda i: ("o", i // L.U), k, it)
                    f = (lambda i: i // 2 + 1) if n == 0 else (lambda i: i + 1)
                    pe.wait_ge(s["a_hi"], at(L, f, k, it))
                    pe.wait_ge(s["a_lo"], at(L, f, k, it))
                    for j, b in enumerate(L.batches(k)):
                        if j not in tiles:
                            continue
                        no = L.tile[(k, b)]
                        if no > 2:
                            pe.wait_ge(s["x_acc"], at(L, lambda i: L.tile[(i, L.batches(i)[j])] - 2, k, it))
                        a = buf["a_hi"][:, tokens(j)], buf["a_lo"][:, tokens(j)]
                        mm3(O[no % 2][:, :], a, ring(c), True, True, last=True).then_inc(s["outp"], 1)
                    if k % L.U == L.U - 1 and len(L.batches(k)) - 1 in tiles:
                        owed[0] += 1

                def step(k, it):
                    if k < L.NU:
                        scores(k, it)
                    if n < 3 and L.NU - 1 <= k <= L.NU:
                        early(n + 1, k - (L.NU - 1))
                    if 1 <= k <= L.NU and n:
                        turn(k - 1, it)
                    for no, (kind, hf, kt, kts) in enumerate(L.parts(k)):
                        if n == 2 and L.has_O(k):
                            output(k - L.lag_o, it, range(2 * no, 2 * no + 2))
                        def what_f(i, kind=kind, hf=hf):
                            return (kind, i // L.U + 1, hf)
                        what = what_f(k)
                        done = kt + kts == KT
                        c = chunk(lambda i: what_f(i)[:2], k, it)
                        if kt == 0:
                            bank_free(what_f, k, it)
                        m = by_feature(dst(what), c, "x" if kind == "q" else "c", hf,
                                       range(kt, kt + kts), last=done)
                        if done:
                            m.then_inc(s["proj"], 1)
                            if hf == 1:
                                owed[0] += 1
                        if n == 1 and L.has_O(k):
                            output(k - L.lag_o, it, range(2 * no, 2 * no + 2))
                    if 1 <= k <= L.NU and not n:
                        turn(k - 1, it)
                    if L.has_O(k) and not (n in (1, 2) and L.parts(k)):
                        output(k - L.lag_o, it)
                    if L.has_V(k):
                        values(k - L.lag_v, it)
                    if n == 2:
                        for what in L.pieces(k):
                            q_squares(lambda i: L.pieces(i)[0], k, it)
                    for j, what in enumerate(L.value_pieces(k)):
                        def what_f(i, j=j):
                            return L.value_pieces(i)[j]
                        bank_free(what_f, k, it)
                        c = chunks(lambda i: what_f(i)[:2], k, it)
                        by_token(dst(what), c, "c", what[2], last=True).then_inc(s["proj"], 1)
                        if what[2] == B - 1:
                            owed[0] += KT

                run_steps(pe, L, step)

            def f_chunk(n, c):
                no = CHUNK_AT[(f"F{n}", c)]
                pe.wait_ge(w_done, no + 1)
                return no

            def all_norm_tiles(n):
                for b in range(B):
                    norm_tile(n, b)

            def mixture(n):
                s, buf, norm = FS[n], MIX[n], 2 * n + 1
                def piece(no, what, t):
                    c = f_chunk(n, (what,))
                    wait_norm(norm, (t + 1) * (B // 2))
                    if no == 2:
                        pe.wait_ge(AS[n + 1]["j_out"], ATT[n + 1].early)
                    by_feature((S + J)[no][:, :], c, "x", t, last=True).then_inc(s["proj"], 1)
                    owed[0] += t

                def turn_weights():
                    pe.wait_ge(s["sx"], 1)
                    for t in range(2):
                        for j in range(4):
                            m = pe.transpose(TV[t][:, tokens(j)], buf["sx"][:, 4 * t + j, :], ident[:, :])
                            if j < 3:
                                told(m)
                        m.then_inc(s["s_turned"], 1)

                for kind, i in NORM_ORDER[n]:
                    if kind == "early":
                        early(n + 1, i)
                    elif kind == "ln":
                        norm_tile(norm, i)
                    else:
                        piece(i, kind, i)
                pe.wait_ge(s["low"], 2)
                for b in range(B):
                    m = pe.transpose(T[:, 8 * b:8 * b + 8], buf["lowT" if n else "lgT"][LOGITS[n], tokens(b)],
                                     ident[LOGITS[n], LOGITS[n]])
                m.then_inc(s["l_turned"], 1)
                if n == 0:
                    for t in range(2):
                        piece(2 + t, "A", t)
                outs = 0
                if n == 1:
                    cs = [f_chunk(1, ("W", kt)) for kt in range(KT)]
                    for b in range(B):
                        if b == DENSE_AHEAD:
                            turn_weights()
                        if b >= 2:
                            pe.wait_ge(s["x_acc"], b - 1)
                        by_token(O[b % 2][:, :], cs, "x", b, last=True).then_inc(s["outp"], 1)
                    owed[0] += KT
                    outs = B
                else:
                    turn_weights()
                c = f_chunk(n, ("B",))
                for b in range(B):
                    pe.wait_ge(s["h_hi"], b // 4 + 1)
                    pe.wait_ge(s["h_lo"], b // 4 + 1)
                    if outs + b >= 2:
                        pe.wait_ge(s["x_acc"], outs + b - 1)
                    h = buf["h_hi"][:, tokens(b)], buf["h_lo"][:, tokens(b)]
                    mm3(O[b % 2][:, :], h, ring(c), True, True, last=True).then_inc(s["outp"], 1)
                owed[0] += 1

            def swiglu():
                s, norm = FS[2], 5
                for kind, i in NORM_ORDER[2]:
                    if kind == "early":
                        early(3, i)
                    elif kind == "ln":
                        norm_tile(norm, i)
                    else:
                        c = f_chunk(2, ("A",))
                        wait_norm(norm, (i + 1) * (B // 2))
                        by_feature(S[i][:, :], c, "x", i, last=True).then_inc(s["proj"], 1)
                        owed[0] += i
                pe.wait_ge(AS[3]["j_out"], ATT[3].early)
                def stacked(dst, weights, low, weights_stand, start, stop):
                    for no, w in enumerate(weights):
                        l, r = (w, low) if weights_stand else (low, w)
                        m = mm(dst, l, r, start and no == 0, stop and no == 1)
                        if not (stop and no == 1):
                            told(m)
                    return m

                def gate_or_up(j, t, w):
                    no = 2 * j + t
                    lora, c = f_chunk(2, ("l", j)), f_chunk(2, ("gu"[w], j))
                    if w == 0 and no >= 2:
                        pe.wait_ge(s["hid"], no - 1)
                    if j == 0:
                        pe.wait_ge(s["low_lo"], t + 1)
                    dst = (J if t == 0 else S)[w][:, :]
                    stacked(dst, ring(lora, tokens(w)), M2["low"][:, half(t)], True, True, False)
                    for kt in range(KT):
                        last = kt == KT - 1
                        m = mm3(dst, ring(c, tokens(kt)), acts("x", kt, half(t)), False, last, last)
                    m.then_inc(s["proj"], 1)
                    owed[0] += t

                def down_low(j):
                    lora, last = f_chunk(2, ("l", j)), j == HIDDEN_TILES - 1
                    for t in range(2):
                        pe.wait_ge(s["h_hi"], 2 * j + t + 1)
                        pe.wait_ge(s["h_lo"], 2 * j + t + 1)
                        h = M2["h_hi"][:, j % 2, half(t)], M2["h_lo"][:, j % 2, half(t)]
                        m = mm3(TV[t][:, :], ring(lora, tokens(2)), h, j == 0, last, last)
                        if last:
                            m.then_inc(s["dl"], 1)
                        owed[0] += t

                def down(j, tiles):
                    d = f_chunk(2, ("d", j))
                    for b in tiles:
                        no = j * B + b + 1
                        if no > 2:
                            pe.wait_ge(s["x_acc"], no - 2)
                        h = M2["h_hi"][:, j % 2, tokens(b)], M2["h_lo"][:, j % 2, tokens(b)]
                        mm3(O[b % 2][:, :], h, ring(d), True, True, last=True).then_inc(s["outp"], 1)
                    if B - 1 in tiles:
                        owed[0] += 1

                for j in range(HIDDEN_TILES):
                    for no, (t, w) in enumerate(((0, 0), (0, 1), (1, 0), (1, 1))):
                        gate_or_up(j, t, w)
                        if j and no == 0:
                            down_low(j - 1)
                        if j:
                            down(j - 1, range(2 * no, 2 * no + 2))
                down_low(HIDDEN_TILES - 1)
                down(HIDDEN_TILES - 1, range(B))
                c = f_chunk(2, ("b",))
                for b in range(B):
                    pe.wait_ge(s["dl_lo"], b // 4 + 1)
                    pe.wait_ge(s["x_acc"], HIDDEN_TILES * B + b - 1)
                    stacked(O[b % 2][:, :], ring(c), M2["dl"][:, tokens(b)], False, True, True)\
                        .then_inc(s["outp"], 1)
                owed[0] += 1

            def quantised():
                s, norm = FS[3], 7
                for i in range(B + 2):
                    if i < B:
                        norm_tile(norm, i)
                    b = i - 2
                    if b < 0:
                        continue
                    wait_norm(norm, b + 1)
                    if b >= 2:
                        pe.wait_ge(s["x_acc"], b - 1)
                    for kt in range(KT):
                        m = mm3(O[b % 2][:, :], acts("x", kt, tokens(b)),
                                (M3["wT_hi"][:, kt, :], M3["wT_lo"][:, kt, :]),
                                kt == 0, kt == KT - 1, kt == KT - 1)
                    m.then_inc(s["outp"], 1)

            attention(0)
            mixture(0)
            attention(1)
            mixture(1)
            attention(2)
            swiglu()
            attention(3)
            quantised()

        @block.scalar
        def _(act):
            def copy(dst, src, scale=None):
                if scale is None:
                    return act.activation(dst, src, ACT.Copy)
                return act.activation(dst, src, ACT.Copy, scale=scale)

            def norm_hi(n, b):
                act.wait_ge(ln_turned, B * n + b + 1)
                copy(xt_hi[:, :, tokens(b)], TV[b % 2][:, :].rearrange("p (k t) -> p k t", k=KT))\
                    .then_inc(ln_hi, 1)

            def early_out(n, no):
                if no == 2:
                    early_out(n, 0)
                    early_out(n, 1)
                L, s, buf = ATT[n], AS[n], BUF[n]
                kind, h, part = what = L.first[no]
                act.wait_ge(s["proj"], no + 1)
                if kind == "k":
                    dst = buf["kT"][:, 0, half(part)]
                elif kind == "Vc":
                    dst = buf["v"][:, 0, part, :]
                else:
                    dst = buf["v"][:, part, 0:D]
                copy(dst, piece_bank(L, what)).then_inc(s["j_out"], 1)

            def attention(n):
                L, s, buf = ATT[n], AS[n], BUF[n]
                phase_start(act, 2 * n)
                if n == 1:
                    act.dma_start(buf["m8"][:, :, :], mask).then_inc(phase_in["L1"], 16)
                    act.dma_start(buf["ln_w"][:, :], ln_weight).then_inc(phase_in["L1"], 16)
                if n == 2:
                    act.dma_start(buf["madd"][:, :], mask_add).then_inc(phase_in["L2"], 16)
                    act.dma_start(buf["qk_w"][:, :], qk_norm).then_inc(phase_in["L2"], 16)
                q_scale_ = {0: 16.0 ** -0.5, 3: float(P) ** -0.5}.get(n)

                def squares(what_f, src, k, it):
                    m = L.rstd[what_f(k)]
                    if 1 < m <= 2 * B + 1:
                        act.wait_ge(s["ksum"], m - 1)
                    elif m > 1:
                        act.wait_ge(s["qss"], at(L, lambda i: L.rstd[what_f(i)] - 1 - 2 * B, k, it))
                    act.activation(buf["sq"][:, :], src, ACT.Square).then_inc(s["sq"], 1)

                def leave_bank(what_f, k, it):
                    what = what_f(k)
                    kind, h, part = what
                    src = piece_bank(L, what)
                    by_tile = src.rearrange("p (b t) -> p b t", b=4)
                    act.wait_ge(s["proj"], at(L, lambda i: L.piece[what_f(i)], k, it))
                    if kind == "K":
                        squares(what_f, src, k, it)
                        return
                    if kind == "q" and n == 2:
                        squares(what_f, src, k, it)
                    scale = None
                    if kind == "q":
                        dst, scale = buf["qT"][:, h % 2, half(part)], q_scale_
                    elif kind == "k":
                        dst = buf["kT"][:, h % 2, half(part)]
                    elif kind == "v0":
                        dst = buf["vT"][:, half(part)]
                    elif kind == "v":
                        dst = buf["v"][:, part, :]
                    elif kind == "V":
                        dst = buf["v"][:, part, h * D:(h + 1) * D]
                    elif kind in ("Kc", "Kx"):
                        o = 0 if kind == "Kc" else P
                        dst, src = buf["kT"][:, h, 4 * part:4 * part + 4, o:o + P], by_tile
                    else:
                        dst = buf["v"][:, 0 if kind == "Vc" else 1, part, :]
                    copy(dst, src, scale).then_inc(s["j_out"], 1)

                def keys_out(what):
                    _, g, b = what
                    act.wait_ge(s["k_turned"], g * B + b + 1)
                    act.wait_ge(s["wqk"], 1)
                    act.activation(buf["kT"][:, 4 * g:4 * g + 4, tokens(b)],
                                   TV[b % 2][:, :].rearrange("p (h t) -> p h t", h=4),
                                   ACT.Copy, scale=buf["qk_w"][:, 0:1]).then_inc(s["k_out"], 1)

                for what in L.first[L.early:]:
                    if what[0] == "ln":
                        norm_hi(2 * n, what[2])
                        continue
                    if what[0] == "w":
                        kt = what[2]
                        act.wait_ge(FS[3]["w_turned"], kt + 1)
                        copy(M3["wT_hi"][:, kt, :], S[kt % 2][:, :]).then_inc(FS[3]["wT_hi"], 1)
                        if kt == 0:
                            act.wait_ge(FS[3]["wn"], 4)
                            act.dma_start(M3["bias"][:, :], q_bias).then_inc(phase_in["F3"], 16)
                        continue
                    leave_bank(lambda i: what, 0, None)
                    if what == ("Kc", 3, 1):
                        act.dma_start(M3["qw"][:, :, :], qweight).then_inc(phase_in["F3"], 16)
                        act.dma_start(M3["sc"][:, :], q_scale).then_inc(phase_in["F3"], 16)
                        act.dma_start(M3["zp"][:, :], q_zero).then_inc(phase_in["F3"], 16)
                    if n == 2 and B + KEY_LAG < L.piece[what] <= B + KEY_LAG + 2 * B:
                        keys_out(L.first[L.piece[what] - KEY_LAG - 1])
                    if what == ("v0", 0, 1):
                        act.wait_ge(s["vt"], 1)
                        for t in range(2):
                            copy(buf["v"][:, 4 * t:4 * t + 4, :], TV[t][:, :].rearrange("p (b t) -> p b t", b=4))\
                                .then_inc(s["v_rows"], 1)

                def turned_out(k, it):
                    if 1 <= k <= L.NU:
                        act.wait_ge(s["turned"], at(L, lambda i: i, k, it))
                        copy(buf["pT"][:, (k - 1) % 2 if n == 0 else 0, :], T[:, :]).then_inc(s["pT"], 1)

                def step(k, it):
                    if n:
                        turned_out(k, it)
                    if k < L.NU:
                        act.wait_ge(s["top"], at(L, lambda i: i + 1, k, it))
                        if k >= 2 and n in (0, 3):
                            act.wait_ge(s["turned"], at(L, lambda i: i - 1, k, it))
                        blocks = 2 if n == 3 else 4
                        w = D // blocks
                        src = S[k % 2] if n in (0, 3) else probs[:, k % 2, :]
                        for j in range(blocks):
                            cols = slice(j * w, (j + 1) * w)
                            e = act.activation(probs[:, k % 2, cols], src[:, cols], ACT.Exp,
                                               bias=top[:, k % 2, j:j + 1], scale=1.0,
                                               accum_out=sums[:, k % 2, j:j + 1])
                        e.then_inc(s["exp"], 1)
                    if n == 0:
                        turned_out(k, it)
                    per = {2: 4 * L.U, 3: 8 * L.U}.get(n, 0)
                    if per and k % per == 1 and k < L.NU:
                        if k > 1:
                            act.wait_ge(s["values"], at(L, lambda i: i - 1, k, it))
                        kv = at(L, lambda i: i // per, k, it)
                        cols = bass.ds(kv * P, P)
                        if n == 2:
                            copy(buf["vc"][:, :, :], buf["v"][:, :, cols]).then_inc(s["vc"], 1)
                        else:
                            copy(buf["vc"][:, :, :, :].rearrange("p a b d -> p (a b) d"),
                                 buf["v"][:, :, :, :].rearrange("p a b d -> p (a b) d")[:, :, cols])\
                                .then_inc(s["vc"], 1)
                    for j in range(len(L.pieces(k))):
                        leave_bank(lambda i, j=j: L.pieces(i)[j], k, it)
                    u = k - L.lag_v
                    if L.has_V(k) and not (n == 0 and u % 2 == 0):
                        act.wait_ge(s["values"], at(L, lambda i: i - L.lag_v + 1, k, it))
                        w = L.nb * P
                        o = u // 2 % 2 * P if n == 0 else 0
                        copy(buf["a_hi"][:, 0:w], V[:, o:o + w]).then_inc(s["a_hi"], 1)
                    for j in range(len(L.value_pieces(k))):
                        leave_bank(lambda i, j=j: L.value_pieces(i)[j], k, it)

                run_steps(act, L, step)

            def mixture(n):
                s, buf, norm = FS[n], MIX[n], 2 * n + 1
                phase_start(act, norm)
                if n == 0:
                    act.dma_start(buf["ex"][:, :], lora_bias).then_inc(phase_in["F0"], 16)
                def low_out(no):
                    act.wait_ge(s["proj"], no + 1)
                    copy(buf["lgT" if n == 0 and no < 2 else "lowT"][:, half(no % 2)], (S + J)[no][:, :]).then_inc(s["low"], 1)

                for kind, i in NORM_ORDER[n]:
                    if kind == "early":
                        early_out(n + 1, i)
                    elif kind == "ln":
                        norm_hi(norm, i)
                    else:
                        low_out(i)
                act.wait_ge(s["probs"], 1)
                act.activation(buf["pr"][:, :, :], buf["pr"][:, :, :], ACT.Exp).then_inc(s["s_exp"], 1)
                if n == 0:
                    low_out(2)
                    low_out(3)
                for t in range(2):
                    act.wait_ge(s["hm"], t + 1)
                    copy(buf["h_hi"][:, half(t)], buf["hm"][:, half(t)]).then_inc(s["h_hi"], 1)

            def swiglu():
                s, norm = FS[2], 5
                phase_start(act, norm)
                for kind, i in NORM_ORDER[2]:
                    if kind == "early":
                        early_out(3, i)
                    elif kind == "ln":
                        norm_hi(norm, i)
                    else:
                        act.wait_ge(s["proj"], i + 1)
                        copy(M2["low"][:, half(i)], S[i][:, :]).then_inc(s["low_hi"], 1)
                for j in range(HIDDEN_TILES):
                    for t in range(2):
                        no = 2 * j + t
                        act.wait_ge(s["proj"], 2 + 2 * no + 1)
                        if no >= 2:
                            act.wait_ge(s["hid"], no - 1)
                        act.activation(M2["sg"][:, t, :], (J if t == 0 else S)[0][:, :], ACT.Silu)\
                            .then_inc(s["silu"], 1)
                        act.wait_ge(s["hid"], no + 1)
                        if j >= 2:
                            act.wait_ge(s["outp"], (j - 1) * B)
                        copy(M2["h_hi"][:, j % 2, half(t)], M2["hid"][:, t, :]).then_inc(s["h_hi"], 1)
                for t in range(2):
                    act.wait_ge(s["dl"], t + 1)
                    copy(M2["dl"][:, half(t)], TV[t][:, :]).then_inc(s["dl_hi"], 1)

            def quantised():
                s, norm = FS[3], 7
                for b in range(B):
                    norm_hi(norm, b)

            for kt in range(KT):
                act.dma_start(A0["ctx_raw"][:, kt, :], ctx_t[kt]).then_inc(ctx_in[kt], 16)
            act.dma_start(gate[:, :], gates).then_inc(gate_in, 16)
            for t in range(2):
                tiles = slice(4 * t, 4 * t + 4)
                act.dma_start(x[:, tiles, :], x_in[tiles].rearrange("b p d -> p b d")).then_inc(x_in_s[t], 16)
            for kt in range(KT):
                act.wait_ge(ctx_in[kt], 16)
                copy(ct_hi[:, kt, :], A0["ctx_raw"][:, kt, :]).then_inc(ctx_hi_done, 1)
            act.wait_ge(gate_in, 16)
            act.activation(gate[:, :], gate[:, :], ACT.Tanh).then_inc(gate_done, 1)
            act.wait_ge(ctx_done, KT)
            act.dma_start(A1["pb"][:, :, :], position_bias).then_inc(pb_in, 16)
            attention(0)
            mixture(0)
            attention(1)
            mixture(1)
            attention(2)
            swiglu()
            attention(3)
            quantised()

        @block.vector
        def _(dve):
            def rsqrt_step(j, v, y, t):
                if j == 0:
                    return dve.tensor_scalar(t.bitcast(I32), v.bitcast(I32), 1, None, ALU.logical_shift_right)
                if j == 1:
                    return dve.tensor_scalar(y.bitcast(I32), t.bitcast(I32), -1.0, float(0x5F3759DF),
                                             ALU.mult, ALU.add)
                if j % 3 == 2:
                    return dve.tensor_tensor(t, y, y, ALU.mult)
                if j % 3 == 0:
                    return dve.scalar_tensor_tensor(out=t, in0=t, scalar=-0.5, in1=v, op0=ALU.mult, op1=ALU.mult)
                return dve.scalar_tensor_tensor(out=y, in0=t, scalar=1.5, in1=y, op0=ALU.add, op1=ALU.mult)

            def rsqrt(v, y, t, sem_, base, final):
                for j in range(RSQRT):
                    if j:
                        dve.wait_ge(sem_, base + j)
                    last = final is not None and j == RSQRT - 1
                    rsqrt_step(j, v, y, t).then_inc(final if last else sem_, 1)
                if final is None:
                    dve.wait_ge(sem_, base + RSQRT)

            LN_STEPS = 2 * B + 1 + RSQRT

            def tile_stats(n, b):
                if n == 0:
                    dve.wait_ge(x_in_s[b // 4], 16)
                elif n % 2:
                    L = ATT[n // 2]
                    dve.wait_ge(AS[n // 2]["x_acc"], max(t for (u, tb), t in L.tile.items() if tb == b))
                else:
                    dve.wait_ge(*ADDS[n - 1])
                dve.bn_stats(stats[:, b, :], x[:, b, :]).then_inc(ln_tiny, 1)

            def norm_stats(n, tiles=range(B)):
                for b in tiles:
                    tile_stats(n, b)
                norm_scale(range(B), LN_STEPS * n + B)

            def norm_scale(tiles, done):
                dve.wait_ge(ln_tiny, done)
                for b in tiles:
                    dve.bn_aggr(mv[:, b, :], stats[:, b, :]).then_inc(ln_tiny, 1)
                done = done + len(tiles)
                some = slice(tiles[0], tiles[-1] + 1)
                dve.wait_ge(ln_tiny, done)
                dve.tensor_scalar(nt[:, 0, some], mv[:, some, 1], EPS, None, ALU.add).then_inc(ln_tiny, 1)
                dve.wait_ge(ln_tiny, done + 1)
                rsqrt(nt[:, 0, some], rstd[:, some], nt[:, 1, some], ln_tiny, done + 1, None)

            def norm_rows(n, b):
                if b >= 2:
                    dve.wait_ge(ln_turned, B * n + b - 1)
                dve.tensor_scalar(probs[:, b % 2, :], x[:, b, :], mv[:, b, 0:1], rstd[:, b:b + 1],
                                  ALU.subtract, ALU.mult).then_inc(ln_rows, 1)

            def norm_lo(n, b):
                dve.wait_ge(ln_hi, B * n + b + 1)
                dve.tensor_tensor(xt_lo[:, :, tokens(b)], TV[b % 2][:, :].rearrange("p (k t) -> p k t", k=KT),
                                  f32(xt_hi[:, :, tokens(b)]), ALU.subtract).then_inc(ln_lo, 1)

            def attention(n):
                L, s, buf = ATT[n], AS[n], BUF[n]
                norm = 2 * n
                g = gate[:, n:n + 1]
                if n == 0:
                    for kt in range(KT):
                        dve.wait_ge(ctx_hi_done, kt + 1)
                        dve.tensor_tensor(ct_lo[:, kt, :], buf["ctx_raw"][:, kt, :], f32(ct_hi[:, kt, :]),
                                          ALU.subtract).then_inc(ctx_done, 1)
                    dve.wait_ge(setup_done, SETUP)
                if n == 2:
                    dve.wait_ge(phase_in["L2"], 32)
                    dve.scalar_tensor_tensor(out=buf["qk_w"][:, 0:1], in0=buf["qk_w"][:, 0:1],
                                             scalar=float(P) ** 0.5, in1=buf["qk_w"][:, 1:2],
                                             op0=ALU.mult, op1=ALU.mult).then_inc(s["wqk"], 1)

                def key_rows(what):
                    m = L.rstd[what]
                    pair, second = (m - 1) // 2, (m - 1) % 2
                    dve.wait_ge(s["sq"], m)
                    dve.tensor_reduce(nt[:, 2, 4 * second:4 * second + 4],
                                      buf["sq"][:, :].rearrange("p (h d) -> p h d", h=4), AX_X, ALU.add)\
                        .then_inc(s["ksum"], 1)
                    if not second:
                        return
                    base = (RSQRT + 1) * pair
                    dve.wait_ge(s["ksum"], m)
                    dve.tensor_scalar(nt[:, 0, :], nt[:, 2, :], P * EPS, None, ALU.add).then_inc(s["newton"], 1)
                    dve.wait_ge(s["newton"], base + 1)
                    rk = buf["rk"][:, pair % 2, :]
                    rsqrt(nt[:, 0, :], rk, nt[:, 1, :], s["newton"], base + 1, None)
                    for j, no in enumerate((m - 1, m)):
                        if no > 2:
                            dve.wait_ge(s["k_turned"], no - 2)
                        dve.tensor_tensor(probs[:, (no - 1) % 2, :].rearrange("p (h d) -> p h d", h=4),
                                          KEY_BANKS[no % 4][:, :].rearrange("p (h d) -> p h d", h=4),
                                          rk[:, 4 * j:4 * j + 4].unsqueeze(2).to_broadcast([P, 4, P]), ALU.mult)\
                            .then_inc(s["rms"], 1)

                def query_rstd(what_f, k, it, steps=(0, RSQRT + 1)):
                    _, h, part = what_f(k)
                    src = J[(L.piece[what_f(k)] + 1) % 2][:, 0:8].rearrange("p (j a) -> p j a", a=2)[:, :, 0]
                    base = at(L, lambda i: newton_base(L, what_f(i)), k, it)
                    for j in range(*steps):
                        if j == 0:
                            dve.wait_ge(s["qss"], at(L, lambda i: L.rstd[what_f(i)] - 2 * B, k, it))
                            o = dve.tensor_scalar(nt[:, 0, 0:4], src, P * EPS, None, ALU.add)
                        else:
                            dve.wait_ge(s["newton"], base + j)
                            o = rsqrt_step(j - 1, nt[:, 0, 0:4], buf["rq"][:, 2 * (h % 2) + part, :],
                                           nt[:, 1, 0:4])
                        o.then_inc(s["rms"] if j == RSQRT else s["newton"], 1)

                def padded_values(k):
                    r, b, hf = k // L.U, L.batches(k)[0], k % 2
                    if k >= 2:
                        dve.wait_ge(s["values"], k - 1)
                    kv = 2 * r + hf
                    dve.wait_ge(s["v_rows"], b // 4 + 1)
                    dve.tensor_copy(buf["vz"][:, k % 2, 112:128], buf["v"][:, b, 16 * kv:16 * kv + 16])\
                        .then_inc(s["vz"], 1)

                def rows(b):
                    norm_rows(norm, b)
                    if n == 1:
                        rms_rows(s, buf, b, g)

                normed = False
                for what in L.first:
                    if what[0] == "K":
                        key_rows(what)
                        if L.rstd[what] % 2 == 0:
                            tile_stats(norm, L.rstd[what] // 2 - 1)
                    elif what == ("w", 0, 0):
                        dequantise()
                    elif what[0] == "w":
                        weight_lo(what[2])
                    elif what[0] == "ln":
                        b = what[2]
                        if not normed:
                            norm_stats(norm, () if n == 2 else range(B))
                            if n == 1:
                                rms_scale(s)
                            if n == 2:
                                dve.wait_ge(s["k_turned"], 2 * B)
                            rows(0)
                            normed = True
                        if b + 1 < B:
                            rows(b + 1)
                        norm_lo(norm, b)
                    elif what[0] == "q" and n == 2:
                        query_rstd(lambda i: what, 0, None)
                if n == 1:
                    dve.wait_ge(phase_in["L1"], 32)
                    dve.tensor_scalar(buf["m"][:, :, :], buf["m8"][:, :, :].bitcast(U8), 1.0, MASKED,
                                      ALU.subtract, ALU.mult).then_inc(s["m_ready"], 1)

                def add_tiles(k, it, tiles=range(B), after=lambda j: None):
                    for j, b in enumerate(L.batches(k - L.lag_o)):
                        if j not in tiles:
                            continue
                        no_f = (lambda i, j=j: L.tile[(i - L.lag_o, L.batches(i - L.lag_o)[j])])
                        dve.wait_ge(s["outp"], at(L, no_f, k, it))
                        if no_f(k) > B:
                            dve.wait_ge(s["x_acc"], at(L, lambda i: no_f(i) - B, k, it))
                        dve.scalar_tensor_tensor(out=x[:, b, :], in0=O[no_f(k) % 2][:, :], scalar=g,
                                                 in1=x[:, b, :], op0=ALU.mult, op1=ALU.add)\
                            .then_inc(s["x_acc"], 1)
                        after(j)

                def tail_stats(k):
                    if L.has_O(k) and k - L.lag_o >= L.NU - L.U:
                        for b in L.batches(k - L.lag_o):
                            tile_stats(norm + 1, b)
                        if n == 3 and k == L.NU:
                            norm_scale(range(B // 2), LN_STEPS * (norm + 1) + 6)
                            norm_rows(norm + 1, 0)
                            norm_rows(norm + 1, 1)

                def step(k, it):
                    def small(a, b=None):
                        if n == 2 and 1 <= k <= L.NU and L.pieces(k - 1):
                            query_rstd(lambda i: L.pieces(i - 1)[0], k, it, (a, b or a + 1))

                    if k < L.NU:
                        h = k // L.U
                        width = L.key_tiles * P
                        rows = D // width
                        bank_ = S[k % 2][:, :].rearrange("p (j t) -> p j t", j=rows)
                        pr = probs[:, k % 2, :].rearrange("p (j t) -> p j t", j=rows)
                        dve.wait_ge(s["scores"], at(L, lambda i: i + 1, k, it))
                        if n in (1, 2) and k >= 2:
                            dve.wait_ge(s["turned"], at(L, lambda i: i - 1, k, it))
                        if n == 1:
                            hh = at(L, lambda i: i // L.U, k, it)
                            pb = buf["pb"][:, hh:hh + 1, :] if it is None else buf["pb"][:, bass.ds(hh, 1), :]
                            dve.tensor_tensor(pr, bank_, pb.to_broadcast([P, 4, P]), ALU.add).then_inc(s["seen"], 1)
                            dve.wait_ge(s["seen"], at(L, lambda i: i + 1, k, it))
                            b0 = L.batches(k)[0]
                            dve.tensor_tensor(pr, pr, buf["m"][:, b0:b0 + 4, :], ALU.add).then_inc(s["masked"], 1)
                            dve.wait_ge(s["masked"], at(L, lambda i: i + 1, k, it))
                            dve.tensor_reduce(top[:, k % 2, :], pr, AX_X, ALU.max, negate=True).then_inc(s["clamp"], 1)
                            dve.wait_ge(s["clamp"], at(L, lambda i: i + 1, k, it))
                            dve.tensor_scalar(top[:, k % 2, :], top[:, k % 2, :], MASKED / 10, None, ALU.min)\
                                .then_inc(s["top"], 1)
                        elif n == 2:
                            dve.wait_ge(s["rms"], at(L, lambda i: L.rstd[("q", i // L.U, i % 2)], k, it))
                            for j in range(4):
                                o = dve.scalar_tensor_tensor(
                                    out=pr[:, j, :], in0=bank_[:, j, :],
                                    scalar=buf["rq"][:, 2 * (h % 2) + k % 2, j:j + 1],
                                    in1=buf["madd"][:, :], op0=ALU.mult, op1=ALU.add)
                                if j == 3:
                                    o.then_inc(s["seen"], 1)
                                small(j)
                            dve.wait_ge(s["seen"], at(L, lambda i: i + 1, k, it))
                            dve.tensor_reduce(top[:, k % 2, :], pr, AX_X, ALU.max, negate=True).then_inc(s["top"], 1)
                        else:
                            dve.tensor_reduce(top[:, k % 2, 0:rows], bank_, AX_X, ALU.max, negate=True)\
                                .then_inc(s["top"], 1)
                        small(4)
                        if n == 0:
                            behind(k, it)
                        if n == 2 and L.has_O(k):
                            add_tiles(k, it, range(2), lambda j: small(5 + j))
                        else:
                            small(5, 7)
                        dve.wait_ge(s["exp"], at(L, lambda i: i + 1, k, it))
                        if n == 1:
                            dve.tensor_scalar(sums[:, k % 2, :], sums[:, k % 2, :], 1e-30, None, ALU.max)\
                                .then_inc(s["sum"], 1)
                            dve.wait_ge(s["sum"], at(L, lambda i: i + 1, k, it))
                        dve.reciprocal(inv[:, k % 2, 0:rows], sums[:, k % 2, 0:rows]).then_inc(s["inv"], 1)
                        small(7)
                        dve.wait_ge(s["inv"], at(L, lambda i: i + 1, k, it))
                        dve.tensor_tensor(pr, pr, inv[:, k % 2, 0:rows].unsqueeze(2).to_broadcast([P, rows, width]),
                                          ALU.mult).then_inc(s["probs"], 1)
                        small(8)
                    elif n == 0:
                        behind(k, it)
                    if n:
                        through(k, it, small)

                def behind(k, it):
                    if 1 <= k <= L.NU:
                        padded_values(k - 1)
                    if k:
                        through(k - 1, it)

                def through(k, it, small=lambda a, b=None: None):
                    if L.has_O(k):
                        if n == 2 and k < L.NU:
                            add_tiles(k, it, range(2, B), lambda j: small(7 + j))
                        else:
                            add_tiles(k, it)
                    elif n == 2 and k < L.NU:
                        small(9, 11)
                    small(11)
                    u = k - L.lag_v
                    if L.has_V(k) and not (n == 0 and u % 2 == 0):
                        f = (lambda i: (i - L.lag_v) // 2 + 1) if n == 0 else (lambda i: i - L.lag_v + 1)
                        dve.wait_ge(s["a_hi"], at(L, f, k, it))
                        w = L.nb * P
                        o = u // 2 % 2 * P if n == 0 else 0
                        dve.tensor_tensor(buf["a_lo"][:, 0:w], V[:, o:o + w], f32(buf["a_hi"][:, 0:w]),
                                          ALU.subtract).then_inc(s["a_lo"], 1)
                    tail_stats(k)

                if n == 0:
                    dve.wait_ge(gate_done, 1)
                if n == 1:
                    dve.wait_ge(pb_in, 16)
                    dve.wait_ge(s["m_ready"], 1)
                run_steps(dve, L, step)
                if n == 0:
                    behind(L.steps, None)

            def rms_scale(s):
                dve.wait_ge(ln_tiny, LN_STEPS * (LN2 + 1))
                dve.tensor_tensor(nt[:, 1, :], rstd[:, :], rstd[:, :], ALU.mult).then_inc(s["r2"], 1)
                dve.wait_ge(s["r2"], 1)
                dve.tensor_tensor(nt[:, 1, :], nt[:, 1, :], mv[:, :, 1], ALU.mult).then_inc(s["r2"], 1)
                dve.wait_ge(s["r2"], 2)
                dve.tensor_scalar(nt[:, 0, :], nt[:, 1, :], EPS, None, ALU.add).then_inc(s["r2"], 1)
                dve.wait_ge(s["r2"], 3)
                rsqrt(nt[:, 0, :], nt[:, 2, :], nt[:, 1, :], s["r2"], 3, None)

            def rms_rows(s, buf, b, g):
                dve.wait_ge(ln_rows, B * LN2 + b + 1)
                dve.scalar_tensor_tensor(out=x[:, b, :], in0=probs[:, b % 2, :], scalar=g, in1=x[:, b, :],
                                         op0=ALU.mult, op1=ALU.add).then_inc(s["added"], 1)
                if b == 0:
                    dve.wait_ge(phase_in["L1"], 32)
                dve.wait_ge(s["added"], b + 1)
                dve.scalar_tensor_tensor(out=probs[:, b % 2, :], in0=probs[:, b % 2, :],
                                         scalar=nt[:, 2, b:b + 1], in1=buf["ln_w"][:, :],
                                         op0=ALU.mult, op1=ALU.mult).then_inc(ln_y, 1)

            def dequantise():
                s = FS[3]
                dve.wait_ge(phase_in["F3"], 48)
                codes = M3["u"][:, :, :].rearrange("p n (g c) -> p (n g) c", c=4)
                words = M3["qw"][:, :, :].rearrange("p n (g c) -> p (n g) c", c=3)
                for c, (w, shift) in enumerate(((0, 0), (0, 6), (1, 0), (2, 0))):
                    dve.tensor_scalar(codes[:, :, c], words[:, :, w], shift, 63,
                                      ALU.logical_shift_right, ALU.bitwise_and).then_inc(s["codes"], 1)
                dve.wait_ge(s["codes"], 4)
                for nt_ in range(KT):
                    dve.tensor_scalar(M3["wn"][:, nt_, :], M3["u"][:, nt_, :], M3["zp"][:, nt_:nt_ + 1],
                                      M3["sc"][:, nt_:nt_ + 1], ALU.subtract, ALU.mult).then_inc(s["wn"], 1)
                weight_lo(0)

            def weight_lo(kt):
                s = FS[3]
                dve.wait_ge(s["wT_hi"], kt + 1)
                dve.tensor_tensor(M3["wT_lo"][:, kt, :], S[kt % 2][:, :], f32(M3["wT_hi"][:, kt, :]),
                                  ALU.subtract).then_inc(s["wT_lo"], 1)

            def norm_all(n, after=lambda b: None):
                if n < 7:
                    norm_stats(n, ())
                    norm_rows(n, 0)
                for b in range(B):
                    if n == 7 and b + 1 == B // 2:
                        norm_scale(range(B // 2, B), LN_STEPS * n + B + B // 2 + 1 + RSQRT)
                    if b + 1 < B and not (n == 7 and b == 0):
                        norm_rows(n, b + 1)
                    norm_lo(n, b)
                    after(b)

            def mixture(n):
                s, buf, norm = FS[n], MIX[n], 2 * n + 1
                g = gate[:, 4 + n:5 + n]
                norm_all(norm)
                tiny = [0]

                def then(ins):
                    tiny[0] += 1
                    ins.then_inc(s["tiny"], 1)
                    dve.wait_ge(s["tiny"], tiny[0])

                def over_experts(v):
                    return v.unsqueeze(2).to_broadcast([P, B, 8])

                pr, pw, s1, s2 = (buf[k][:, :, :] for k in ("pr", "pw", "s1", "s2"))
                red, red2 = buf["red"][:, 0, :], buf["red"][:, 1, :]
                then(dve.memset(buf["sx"][:, :, :], 0.0))
                if n == 0:
                    dve.wait_ge(phase_in["F0"], 16)
                else:
                    for e in range(8):
                        then(dve.memset(buf["ex"][:, e:e + 1], float(8 - e)))
                dve.wait_ge(s["l_turned"], 1)
                logits = T[:, 0:8 * B].rearrange("p (b e) -> p b e", e=8)
                if n == 0:
                    then(dve.tensor_tensor(pr, logits, buf["ex"][:, :].unsqueeze(1).to_broadcast([P, B, 8]),
                                           ALU.add))
                else:
                    then(dve.tensor_copy(pr, logits))
                then(dve.tensor_reduce(red, pr, AX_X, ALU.max))
                dve.tensor_tensor(pr, pr, over_experts(red), ALU.subtract).then_inc(s["probs"], 1)

                def add_out(no, b, before=None):
                    dve.wait_ge(s["outp"], no)
                    if before:
                        dve.wait_ge(s["x_acc"], before)
                    dve.scalar_tensor_tensor(out=x[:, b, :], in0=O[b % 2][:, :], scalar=g, in1=x[:, b, :],
                                             op0=ALU.mult, op1=ALU.add).then_inc(s["x_acc"], 1)

                dve.wait_ge(s["s_exp"], 1)
                then(dve.tensor_reduce(red, pr, AX_X, ALU.add))
                then(dve.reciprocal(red2, red))
                then(dve.tensor_tensor(pr, pr, over_experts(red2), ALU.mult))
                if n == 0:
                    then(dve.tensor_scalar(pw, pr, 8.0 * 2.0, None, ALU.mult))
                    rank = 16
                else:
                    order = buf["ex"][:, :].unsqueeze(1).to_broadcast([P, B, 8])

                    def pick(sel, tmp):
                        then(dve.tensor_reduce(red, pw, AX_X, ALU.max))
                        then(dve.tensor_tensor(tmp, pw, over_experts(red), ALU.is_equal))
                        then(dve.tensor_tensor(tmp, tmp, order, ALU.mult))
                        then(dve.tensor_reduce(red2, tmp, AX_X, ALU.max))
                        then(dve.tensor_tensor(sel, tmp, over_experts(red2), ALU.is_equal))

                    then(dve.tensor_copy(pw, pr))
                    pick(s1, s2)
                    add_out(1, 0)
                    then(dve.scalar_tensor_tensor(out=pw, in0=s1, scalar=-4.0, in1=pr, op0=ALU.mult, op1=ALU.add))
                    pick(s2, s2)
                    then(dve.tensor_tensor(s1, s1, s2, ALU.add))
                    then(dve.tensor_tensor(pw, pr, s1, ALU.mult))
                    then(dve.tensor_reduce(red, pw, AX_X, ALU.add))
                    then(dve.reciprocal(red2, red))
                    then(dve.tensor_tensor(pw, pw, over_experts(red2), ALU.mult))
                    then(dve.tensor_scalar(pw, pw, 2.0, None, ALU.mult))
                    rank = 8
                for b in range(B):
                    o = dve.tensor_copy(buf["sx"][:, b, 0:8 * rank].rearrange("p (e r) -> p e r", e=8),
                                        pw[:, b, :].unsqueeze(2).to_broadcast([P, 8, rank]))
                o.then_inc(s["sx"], 1)
                outs = 0
                if n == 1:
                    for b in range(1, DENSE_AHEAD):
                        add_out(b + 1, b)
                    outs = B
                dve.wait_ge(s["low"], 2 if n else 4)
                for t in range(2):
                    dve.wait_ge(s["s_turned"], t + 1)
                    dve.tensor_tensor(buf["hm"][:, half(t)], TV[t][:, :], buf["lowT"][:, half(t)], ALU.mult)\
                        .then_inc(s["hm"], 1)
                for t in range(2):
                    dve.wait_ge(s["h_hi"], t + 1)
                    dve.tensor_tensor(buf["h_lo"][:, half(t)], buf["hm"][:, half(t)],
                                      f32(buf["h_hi"][:, half(t)]), ALU.subtract).then_inc(s["h_lo"], 1)
                for b in range(DENSE_AHEAD if n else B, B):
                    add_out(b + 1, b)
                for b in range(B):
                    add_out(outs + b + 1, b, b + 1 if outs else None)

            def swiglu():
                s, norm = FS[2], 5
                g = gate[:, 6:7]
                norm_all(norm)
                def low_parts(what, banks, hi_done, lo_done):
                    for t in range(2):
                        dve.wait_ge(s[hi_done], t + 1)
                        rows = M2[what][32:64, half(t)]
                        dve.tensor_tensor(rows, banks[t][32:64, :], f32(rows), ALU.subtract)\
                            .then_inc(s[lo_done], 1)

                def hidden(j, t):
                    no = 2 * j + t
                    dve.wait_ge(s["silu"], no + 1)
                    dve.wait_ge(s["proj"], 2 + 2 * no + 2)
                    if no >= 2:
                        dve.wait_ge(s["h_hi"], no - 1)
                    dve.tensor_tensor(M2["hid"][:, t, :], (J if t == 0 else S)[1][:, :],
                                      M2["sg"][:, t, :], ALU.mult).then_inc(s["hid"], 1)
                    dve.wait_ge(s["h_hi"], no + 1)
                    dve.tensor_tensor(M2["h_lo"][:, j % 2, half(t)], M2["hid"][:, t, :],
                                      f32(M2["h_hi"][:, j % 2, half(t)]), ALU.subtract)\
                        .then_inc(s["h_lo"], 1)

                def add_tiles(j, tiles):
                    for b in tiles:
                        add_tile(s, g, j * B + b + 1, b)

                low_parts("low", S, "low_hi", "low_lo")
                for j in range(HIDDEN_TILES):
                    if j:
                        add_tiles(j - 1, range(0, 2))
                    hidden(j, 0)
                    if j:
                        add_tiles(j - 1, range(2, 6))
                    hidden(j, 1)
                    if j:
                        add_tiles(j - 1, range(6, B))
                low_parts("dl", TV, "dl_hi", "dl_lo")
                add_tiles(HIDDEN_TILES - 1, range(B))
                add_tiles(HIDDEN_TILES, range(B))

            def add_tile(s, g, no, b):
                dve.wait_ge(s["outp"], no)
                if no > B:
                    dve.wait_ge(s["x_acc"], no - B)
                dve.scalar_tensor_tensor(out=x[:, b, :], in0=O[b % 2][:, :], scalar=g, in1=x[:, b, :],
                                         op0=ALU.mult, op1=ALU.add).then_inc(s["x_acc"], 1)

            def quantised():
                s, norm = FS[3], 7
                g = gate[:, 7:8]
                dve.wait_ge(phase_in["F3"], 64)

                def add(b):
                    dve.wait_ge(s["outp"], b + 1)
                    dve.wait_ge(s["biased"], b + 1)
                    dve.scalar_tensor_tensor(out=x[:, b, :], in0=O[b % 2][:, :], scalar=g, in1=x[:, b, :],
                                             op0=ALU.mult, op1=ALU.add).then_inc(s["x_acc"], 1)

                def after(b):
                    dve.scalar_tensor_tensor(out=x[:, b, :], in0=M3["bias"][:, :], scalar=g, in1=x[:, b, :],
                                             op0=ALU.mult, op1=ALU.add).then_inc(s["biased"], 1)
                    if b >= 2:
                        add(b - 2)

                norm_all(norm, after)
                for b in range(B - 2, B):
                    add(b)

            attention(0)
            mixture(0)
            attention(1)
            mixture(1)
            attention(2)
            swiglu()
            attention(3)
            quantised()


def by_feature_chunk(w_t, m, width=P):
    out = np.zeros((P, KT, P), w_t.dtype)
    out[:, :, :width] = w_t[:, m * width:(m + 1) * width].reshape(KT, P, width).transpose(1, 0, 2)
    return out.reshape(P, D)


def by_token_chunk(w_t, g, kt):
    return w_t[kt * P:(kt + 1) * P, g * D:(g + 1) * D]


def rows_chunk(w, r):
    out = np.zeros((P, D), w.dtype)
    part = w[r * P:(r + 1) * P]
    out[:len(part)] = part
    return out


def lay_out_stream(a):
    t = {k: np.ascontiguousarray(v.T) for k, v in a.items() if k in (
        "L1_xattn_w_q", "L1_xattn_w_k", "L1_xattn_w_v", "L1_xattn_w_out", "L2_xattn_q_proj_w",
        "L2_xattn_k_proj_w", "L2_xattn_v_proj_w", "L2_xattn_o_proj_w", "L1_ffn_W_base", "L0_ffn_Wr",
        "L1_ffn_gate_W", "L2_ffn_gate_w", "L2_ffn_up_w", "L2_ffn_down_w", "L2_ffn_gate_a",
        "L2_ffn_up_a", "L2_ffn_down_a", "L2_ffn_gate_b", "L2_ffn_up_b", "L2_ffn_down_b")}
    wk_rep = np.repeat(a["L0_xattn_Wk"].reshape(D, 8, 1, 16), 4, axis=2).reshape(D, D)
    low_a = [a[f"L{n}_ffn_A"].reshape(-1, D).T for n in range(2)]
    low_b = [a[f"L{n}_ffn_B"].transpose(0, 2, 1).reshape(-1, D) for n in range(2)]

    def chunk(phase, c):
        kind, i = c[0], c[1:]
        if phase == "L0":
            w = {"q": a["L0_xattn_Wq"], "k": wk_rep, "v0": a["L0_xattn_Wv"]}
            return rows_chunk(a["L0_xattn_Wo"], i[0]) if kind == "o" else by_feature_chunk(w[kind], i[0])
        if phase == "L1":
            if kind == "v":
                return by_token_chunk(t["L1_xattn_w_v"], *i)
            if kind == "o":
                return rows_chunk(t["L1_xattn_w_out"], i[0])
            return by_feature_chunk(t[f"L1_xattn_w_{kind}"], i[0])
        if phase == "L2":
            if kind in ("K", "V"):
                return by_token_chunk(t[f"L2_xattn_{kind.lower()}_proj_w"], *i)
            if kind == "o":
                return rows_chunk(t["L2_xattn_o_proj_w"], i[0])
            return by_feature_chunk(t["L2_xattn_q_proj_w"], i[0])
        if phase == "L3":
            if kind in ("V", "Vc"):
                return by_token_chunk(a["L3_xattn_Wv"], *i)
            if kind == "o":
                return rows_chunk(a["L3_xattn_Wo"], i[0])
            return by_feature_chunk(a[f"L3_xattn_W{kind.lower()}"], i[0])
        if phase in ("F0", "F1"):
            n = int(phase[1])
            if kind == "R":
                return by_feature_chunk(t["L0_ffn_Wr"], 0, 8)
            if kind == "A" and n == 1:
                return by_feature_chunk(np.concatenate([low_a[1], t["L1_ffn_gate_W"]], 1), 0, 72)
            if kind == "A":
                return by_feature_chunk(low_a[0], 0, P)
            if kind == "B":
                return rows_chunk(low_b[n], 0)
            return by_token_chunk(t["L1_ffn_W_base"], 0, i[0])
        if kind == "A":
            return by_feature_chunk(np.concatenate([t["L2_ffn_gate_a"], t["L2_ffn_up_a"]] * 2, 1), 0, 64)
        if kind == "b":
            return rows_chunk(np.concatenate([t["L2_ffn_down_b"], zeros, t["L2_ffn_down_b"]]), 0)
        j = i[0]
        n = min(P, t["L2_ffn_gate_w"].shape[1] - j * P)
        cols = slice(j * P, j * P + n)
        if kind in ("g", "u"):
            w = t["L2_ffn_gate_w" if kind == "g" else "L2_ffn_up_w"]
            return by_feature_chunk(w[:, cols], 0, n)
        if kind == "d":
            return rows_chunk(t["L2_ffn_down_w"], j)
        out = np.zeros((P, D), w_dtype)
        for r in (0, 32):
            out[r:r + 16, 0:n] = t["L2_ffn_gate_b"][:, cols]
            out[r + 16:r + 32, P:P + n] = t["L2_ffn_up_b"][:, cols]
            out[0:n, 2 * P + r:2 * P + r + 16] = t["L2_ffn_down_a"][cols, :]
        return out

    w_dtype = a["L0_xattn_Wq"].dtype
    zeros = np.zeros((16, D), w_dtype)
    stream = np.zeros((STREAM_LEN, P, D), w_dtype)
    for no, (phase, c) in enumerate(STREAM):
        stream[no] = chunk(phase, c)
    return stream


def kernel(**inputs):
    import concourse.bacc as bacc
    from concourse.bass_utils import run_bass_kernel_spmd

    a = {k: np.asarray(v) for k, v in inputs.items()}

    def rows(v):
        return np.ascontiguousarray(np.broadcast_to(v.reshape(1, -1), (P, v.size)))

    arrays = {
        "x_in": a["x"],
        "ctx_t": np.ascontiguousarray(a["ctx_4096"].reshape(TOK, D).T.reshape(KT, P, TOK)),
        "mask": np.ascontiguousarray(a["mask_BxSxS2_bk0"].transpose(1, 0, 2)).view(np.uint32),
        "mask_add": a["mask_1x1xSxS2_ff0"].reshape(P, P),
        "gates": rows(np.concatenate([a["g_xattn"], a["g_ffn"]])),
        "stream": lay_out_stream(a),
        "lora_bias": rows(a["L0_ffn_br"]),
        "position_bias": np.ascontiguousarray(a["L1_xattn_position_bias"].transpose(1, 0, 2)),
        "ln_weight": rows(a["L1_xattn_ln_weight"]),
        "qk_norm": np.ascontiguousarray(np.stack([a["L2_xattn_q_norm_w"], a["L2_xattn_k_norm_w"]], 1)),
        "qweight": np.ascontiguousarray(a["L3_ffn_qweight"].reshape(KT, P, 384).transpose(1, 0, 2)),
        "q_scale": np.ascontiguousarray(a["L3_ffn_weight_scale"].reshape(KT, P).T),
        "q_zero": np.ascontiguousarray(a["L3_ffn_weight_zero_point"].reshape(KT, P).T),
        "q_bias": rows(a["L3_ffn_bias"]),
    }
    nc = bacc.Bacc("TRN2", target_bir_lowering=False, num_devices=1)
    arrays = {f"in_{k}": np.ascontiguousarray(v) for k, v in arrays.items()}
    args = [nc.dram_tensor(k, v.shape, mybir.dt.from_np(v.dtype), kind="ExternalInput").ap()
            for k, v in arrays.items()]
    out = nc.dram_tensor("out_0", (B, P, D), F32, kind="ExternalOutput").ap()
    build(nc, *args, out)
    r = run_bass_kernel_spmd(nc, [arrays], core_ids=[0])
    return r.results[0]["out_0"]
```
